# Optimizing a Trainium2 kernel written in Bass

```python
import numpy as np
import jax
import jax.numpy as jnp

def _softmax(x, axis=-1):
    return jax.nn.softmax(x, axis=axis)

def _gelu(x):
    return jax.nn.gelu(x, approximate=True)

def _silu(x):
    return jax.nn.silu(x)

def _sigmoid(x):
    return jax.nn.sigmoid(x)

def _layernorm(x, axis=-1, eps=1e-05):
    m = jnp.mean(x, axis=axis, keepdims=True)
    v = jnp.var(x, axis=axis, keepdims=True)
    return (x - m) / jnp.sqrt(v + eps)

def _scatter_add(tgt, idx, src, axis=0):
    return tgt.at[idx].add(src)

def _segment_sum(src, seg, n):
    return jax.ops.segment_sum(src, seg, n)
kernel_name = 'mk_adaln_ffn_d1_seqx_r2_35e75b'

def setup_inputs(seed: int=0):
    np.random.seed(seed)
    _w = jnp.asarray

    def _rec_inputs():
        import jax
        import jax.numpy as jnp
        _rk = jax.random.key(seed)
        x = -5.722e-05 + 0.9998 * jax.random.normal(jax.random.fold_in(_rk, 1), (2, 2048, 512), jnp.float32)
        _lenS = 2048 - jax.random.randint(jax.random.fold_in(_rk, 7), (2,), 0, max(1, 2048 // 4) + 1, jnp.int32)
        _lenS2 = 2048 - jax.random.randint(jax.random.fold_in(_rk, 8), (2,), 0, max(1, 2048 // 4) + 1, jnp.int32)
        cond_1024 = -0.0142567 + 1.00875 * jax.random.normal(jax.random.fold_in(_rk, 11), (2, 512), jnp.float32)
        return (x, cond_1024)
    x, cond_1024 = _rec_inputs()

    def _L0_cond_setup():
        import jax, jax.numpy as jnp
        import numpy as np
        MODEL_DIM = 512
        NUM_HEADS = 16
        HEAD_DIM = MODEL_DIM // NUM_HEADS
        BATCH = 16
        KEY_LEN = 2048
        key = jax.random.key(seed)
        ks = jax.random.split(key, 10)
        u = lambda k, shape: jax.random.uniform(k, shape, jnp.float32, -0.5, 0.5)
        return {'hidden_states': jax.random.normal(ks[0], (BATCH, 1, MODEL_DIM), jnp.float32), 'key_value_states': jax.random.normal(ks[1], (BATCH, KEY_LEN, MODEL_DIM), jnp.float32), 'Wq': u(ks[2], (MODEL_DIM, MODEL_DIM)), 'bq': u(ks[3], (MODEL_DIM,)), 'Wk': u(ks[4], (MODEL_DIM, MODEL_DIM)), 'bk': u(ks[5], (MODEL_DIM,)), 'Wv': u(ks[6], (MODEL_DIM, MODEL_DIM)), 'bv': u(ks[7], (MODEL_DIM,)), 'Wo': u(ks[8], (MODEL_DIM, MODEL_DIM)), 'bo': u(ks[9], (MODEL_DIM,))}
    _L0_cond_all = _L0_cond_setup()
    _L0_cond_in = {k: v for k, v in _L0_cond_all.items() if k in ('Wq', 'bq', 'Wk', 'bk', 'Wv', 'bv', 'Wo', 'bo')}
    del _L0_cond_all

    def _L0_ffn_setup():
        import jax, jax.numpy as jnp
        import numpy as np
        DIM = 512
        DEPTH = 2
        HEADS = 8
        DIM_HEAD = 64
        WINDOW = 256
        INNER = HEADS * DIM_HEAD
        HID = int(DIM * 4 * 2 / 3)
        B, N = (2, 4096)
        QK_SCALE = 8.0

        def shift_token(t):
            t1, t2 = jnp.split(t, 2, axis=-1)
            t2 = jnp.pad(t2, ((0, 0), (1, 0), (0, 0)))[:, :-1]
            return jnp.concatenate([t1, t2], axis=-1)

        def l2norm(t):
            return t / jnp.clip(jnp.linalg.norm(t, axis=-1, keepdims=True), 1e-12)

        def rotate_half(x):
            x1, x2 = jnp.split(x, 2, axis=-1)
            return jnp.concatenate([-x2, x1], axis=-1)

        def rotary_xpos(q, k):
            n = q.shape[-2]
            half_idx = jnp.arange(0, DIM_HEAD, 2, dtype=jnp.float32)
            inv_freq = 1.0 / 10000.0 ** (half_idx / DIM_HEAD)
            t = jnp.arange(n, dtype=jnp.float32)
            freqs = t[:, None] * inv_freq[None, :]
            freqs = jnp.concatenate([freqs, freqs], axis=-1)
            base = (half_idx + 0.4 * DIM_HEAD) / (1.4 * DIM_HEAD)
            power = (t - n // 2) / float(WINDOW // 2)
            scale = base[None, :] ** power[:, None]
            scale = jnp.concatenate([scale, scale], axis=-1)
            cos, sin = (jnp.cos(freqs), jnp.sin(freqs))
            q = q * cos * scale + rotate_half(q) * sin * scale
            k = k * cos / scale + rotate_half(k) * sin / scale
            return (q, k)

        def local_attention(q, k, v):
            b, h, n, d = q.shape
            w = n // WINDOW
            bq = q.reshape(b, h, w, WINDOW, d) * QK_SCALE
            bk = k.reshape(b, h, w, WINDOW, d)
            bv = v.reshape(b, h, w, WINDOW, d)

            def look_around(t):
                p = jnp.pad(t, ((0, 0), (0, 0), (1, 0), (0, 0), (0, 0)))
                return jnp.concatenate([p[:, :, :w], p[:, :, 1:]], axis=3)
            bk, bv = (look_around(bk), look_around(bv))
            bt = jnp.arange(n).reshape(w, WINDOW)
            btp = jnp.pad(bt, ((1, 0), (0, 0)), constant_values=-1)
            btk = jnp.concatenate([btp[:w], btp[1:]], axis=1)
            sim = jnp.einsum('bhwid,bhwjd->bhwij', bq, bk)
            i = bt[:, :, None]
            j = btk[:, None, :]
            mask = (i < j) | (i > j + WINDOW) | (j == -1)
            sim = jnp.where(mask, -jnp.finfo(sim.dtype).max, sim)
            attn = jax.nn.softmax(sim, axis=-1)
            out = jnp.einsum('bhwij,bhwjd->bhwid', attn, bv)
            return out.reshape(b, h, n, d)

        def _layer(x, wqkv, qs, ksc, wo, lg, lb, w1, b1, w2, b2):
            b, n, _ = x.shape
            h = shift_token(x)
            qkv = h @ wqkv
            q, k, v = jnp.split(qkv, 3, axis=-1)
            to_heads = lambda t: t.reshape(b, n, HEADS, DIM_HEAD).transpose(0, 2, 1, 3)
            q, k, v = (to_heads(q), to_heads(k), to_heads(v))
            q = l2norm(q) * qs
            k = l2norm(k) * ksc
            q, k = rotary_xpos(q, k)
            o = local_attention(q, k, v)
            o = o.transpose(0, 2, 1, 3).reshape(b, n, INNER)
            x = x + o @ wo
            h = shift_token(x)
            mu = h.mean(-1, keepdims=True)
            var = h.var(-1, keepdims=True)
            h = (h - mu) / jnp.sqrt(var + 1e-05) * lg + lb
            h = h @ w1 + b1
            a, g = jnp.split(h, 2, axis=-1)
            h = a * jax.nn.gelu(g, approximate=False)
            x = x + h @ w2 + b2
            return x
        key = jax.random.key(seed)
        ks = jax.random.split(key, 6)
        return {'x': jax.random.normal(ks[0], (B, N, DIM), jnp.float32), 'wqkv': jax.random.normal(ks[1], (DEPTH, DIM, 3 * INNER), jnp.float32) * 0.02, 'q_scale': jnp.ones((DEPTH, DIM_HEAD), jnp.float32), 'k_scale': jnp.ones((DEPTH, DIM_HEAD), jnp.float32), 'wo': jax.random.normal(ks[2], (DEPTH, INNER, DIM), jnp.float32) * 0.02, 'ln_g': jnp.ones((DEPTH, DIM), jnp.float32), 'ln_b': jnp.zeros((DEPTH, DIM), jnp.float32), 'w1': jax.random.normal(ks[3], (DEPTH, DIM, 2 * HID), jnp.float32) * 0.02, 'b1': jnp.zeros((DEPTH, 2 * HID), jnp.float32), 'w2': jax.random.normal(ks[4], (DEPTH, HID, DIM), jnp.float32) * 0.02, 'b2': jnp.zeros((DEPTH, DIM), jnp.float32)}
    _L0_ffn_all = _L0_ffn_setup()
    _L0_ffn_in = {k: v for k, v in _L0_ffn_all.items() if k in ('wqkv', 'q_scale', 'k_scale', 'wo', 'ln_g', 'ln_b', 'w1', 'b1', 'w2', 'b2')}
    del _L0_ffn_all
    return {'x': x, 'cond_1024': cond_1024, 'L0_cond_Wq': _L0_cond_in['Wq'], 'L0_cond_bq': _L0_cond_in['bq'], 'L0_cond_Wk': _L0_cond_in['Wk'], 'L0_cond_bk': _L0_cond_in['bk'], 'L0_cond_Wv': _L0_cond_in['Wv'], 'L0_cond_bv': _L0_cond_in['bv'], 'L0_cond_Wo': _L0_cond_in['Wo'], 'L0_cond_bo': _L0_cond_in['bo'], 'L0_ffn_wqkv': _L0_ffn_in['wqkv'], 'L0_ffn_q_scale': _L0_ffn_in['q_scale'], 'L0_ffn_k_scale': _L0_ffn_in['k_scale'], 'L0_ffn_wo': _L0_ffn_in['wo'], 'L0_ffn_ln_g': _L0_ffn_in['ln_g'], 'L0_ffn_ln_b': _L0_ffn_in['ln_b'], 'L0_ffn_w1': _L0_ffn_in['w1'], 'L0_ffn_b1': _L0_ffn_in['b1'], 'L0_ffn_w2': _L0_ffn_in['w2'], 'L0_ffn_b2': _L0_ffn_in['b2']}

def reference(x, cond_1024, L0_cond_Wq, L0_cond_bq, L0_cond_Wk, L0_cond_bk, L0_cond_Wv, L0_cond_bv, L0_cond_Wo, L0_cond_bo, L0_ffn_wqkv, L0_ffn_q_scale, L0_ffn_k_scale, L0_ffn_wo, L0_ffn_ln_g, L0_ffn_ln_b, L0_ffn_w1, L0_ffn_b1, L0_ffn_w2, L0_ffn_b2):
    import jax
    import jax.numpy as jnp

    def _L0_cond_ref(hidden_states, key_value_states, Wq, bq, Wk, bk, Wv, bv, Wo, bo):
        import jax, jax.numpy as jnp
        import numpy as np
        MODEL_DIM = 512
        NUM_HEADS = 16
        HEAD_DIM = MODEL_DIM // NUM_HEADS
        BATCH = 16
        KEY_LEN = 2048
        B, K = (key_value_states.shape[0], key_value_states.shape[1])
        H, Dh = (NUM_HEADS, HEAD_DIM)
        q = hidden_states @ Wq.T + bq
        k = key_value_states @ Wk.T + bk
        v = key_value_states @ Wv.T + bv
        q = q.reshape(B, 1, H, Dh).transpose(0, 2, 1, 3)
        k = k.reshape(B, K, H, Dh).transpose(0, 2, 1, 3)
        v = v.reshape(B, K, H, Dh).transpose(0, 2, 1, 3)
        q = q / jnp.sqrt(jnp.asarray(Dh, q.dtype))
        scores = jnp.einsum('bhqd,bhkd->bhqk', q, k)[:, :, 0, :]
        attn = jnp.clip(scores, 0.0, 1.0)
        context = attn[..., None] * v
        context = context.transpose(0, 2, 1, 3).reshape(B, K, H * Dh)
        output = context @ Wo.T + bo
        return output

    def _L0_ffn_ref(x, wqkv, q_scale, k_scale, wo, ln_g, ln_b, w1, b1, w2, b2):
        import jax, jax.numpy as jnp
        import numpy as np
        DIM = 512
        DEPTH = 2
        HEADS = 8
        DIM_HEAD = 64
        WINDOW = 256
        INNER = HEADS * DIM_HEAD
        HID = int(DIM * 4 * 2 / 3)
        B, N = (2, 4096)
        QK_SCALE = 8.0

        def shift_token(t):
            t1, t2 = jnp.split(t, 2, axis=-1)
            t2 = jnp.pad(t2, ((0, 0), (1, 0), (0, 0)))[:, :-1]
            return jnp.concatenate([t1, t2], axis=-1)

        def l2norm(t):
            return t / jnp.clip(jnp.linalg.norm(t, axis=-1, keepdims=True), 1e-12)

        def rotate_half(x):
            x1, x2 = jnp.split(x, 2, axis=-1)
            return jnp.concatenate([-x2, x1], axis=-1)

        def rotary_xpos(q, k):
            n = q.shape[-2]
            half_idx = jnp.arange(0, DIM_HEAD, 2, dtype=jnp.float32)
            inv_freq = 1.0 / 10000.0 ** (half_idx / DIM_HEAD)
            t = jnp.arange(n, dtype=jnp.float32)
            freqs = t[:, None] * inv_freq[None, :]
            freqs = jnp.concatenate([freqs, freqs], axis=-1)
            base = (half_idx + 0.4 * DIM_HEAD) / (1.4 * DIM_HEAD)
            power = (t - n // 2) / float(WINDOW // 2)
            scale = base[None, :] ** power[:, None]
            scale = jnp.concatenate([scale, scale], axis=-1)
            cos, sin = (jnp.cos(freqs), jnp.sin(freqs))
            q = q * cos * scale + rotate_half(q) * sin * scale
            k = k * cos / scale + rotate_half(k) * sin / scale
            return (q, k)

        def local_attention(q, k, v):
            b, h, n, d = q.shape
            w = n // WINDOW
            bq = q.reshape(b, h, w, WINDOW, d) * QK_SCALE
            bk = k.reshape(b, h, w, WINDOW, d)
            bv = v.reshape(b, h, w, WINDOW, d)

            def look_around(t):
                p = jnp.pad(t, ((0, 0), (0, 0), (1, 0), (0, 0), (0, 0)))
                return jnp.concatenate([p[:, :, :w], p[:, :, 1:]], axis=3)
            bk, bv = (look_around(bk), look_around(bv))
            bt = jnp.arange(n).reshape(w, WINDOW)
            btp = jnp.pad(bt, ((1, 0), (0, 0)), constant_values=-1)
            btk = jnp.concatenate([btp[:w], btp[1:]], axis=1)
            sim = jnp.einsum('bhwid,bhwjd->bhwij', bq, bk)
            i = bt[:, :, None]
            j = btk[:, None, :]
            mask = (i < j) | (i > j + WINDOW) | (j == -1)
            sim = jnp.where(mask, -jnp.finfo(sim.dtype).max, sim)
            attn = jax.nn.softmax(sim, axis=-1)
            out = jnp.einsum('bhwij,bhwjd->bhwid', attn, bv)
            return out.reshape(b, h, n, d)

        def _layer(x, wqkv, qs, ksc, wo, lg, lb, w1, b1, w2, b2):
            b, n, _ = x.shape
            h = shift_token(x)
            qkv = h @ wqkv
            q, k, v = jnp.split(qkv, 3, axis=-1)
            to_heads = lambda t: t.reshape(b, n, HEADS, DIM_HEAD).transpose(0, 2, 1, 3)
            q, k, v = (to_heads(q), to_heads(k), to_heads(v))
            q = l2norm(q) * qs
            k = l2norm(k) * ksc
            q, k = rotary_xpos(q, k)
            o = local_attention(q, k, v)
            o = o.transpose(0, 2, 1, 3).reshape(b, n, INNER)
            x = x + o @ wo
            h = shift_token(x)
            mu = h.mean(-1, keepdims=True)
            var = h.var(-1, keepdims=True)
            h = (h - mu) / jnp.sqrt(var + 1e-05) * lg + lb
            h = h @ w1 + b1
            a, g = jnp.split(h, 2, axis=-1)
            h = a * jax.nn.gelu(g, approximate=False)
            x = x + h @ w2 + b2
            return x
        for l in range(DEPTH):
            x = _layer(x, wqkv[l], q_scale[l], k_scale[l], wo[l], ln_g[l], ln_b[l], w1[l], b1[l], w2[l], b2[l])
        return x
    x = x + _L0_ffn_ref(_L0_cond_ref(cond_1024[:, None, :], x, L0_cond_Wq, L0_cond_bq, L0_cond_Wk, L0_cond_bk, L0_cond_Wv, L0_cond_bv, L0_cond_Wo, L0_cond_bo), L0_ffn_wqkv, L0_ffn_q_scale, L0_ffn_k_scale, L0_ffn_wo, L0_ffn_ln_g, L0_ffn_ln_b, L0_ffn_w1, L0_ffn_b1, L0_ffn_w2, L0_ffn_b2)
    return x

_drawn_inputs = setup_inputs


def setup_inputs(seed=0):
    import zlib

    import numpy as np

    out = dict(_drawn_inputs(seed))
    spreads = {'L0_ffn_q_scale': (1.0, 0.6),
     'L0_ffn_k_scale': (1.0, 0.6),
     'L0_ffn_ln_g': (1.0, 0.6),
     'L0_ffn_ln_b': (0.0, 0.8),
     'L0_ffn_b1': (0.0, 0.8),
     'L0_ffn_b2': (0.0, 0.8)}
    factors = {'L0_cond_bo': 5.756, 'L0_ffn_w1': 8.0, 'L0_ffn_w2': 8.0}
    for name, (base, spread) in spreads.items():
        noise = np.random.default_rng([zlib.crc32(name.encode()), seed]).standard_normal(out[name].shape)
        drawn = base * np.exp(spread * noise) if base else spread * noise
        out[name] = jnp.asarray(drawn.astype(out[name].dtype))
    for name, factor in factors.items():
        out[name] = (out[name] * factor).astype(out[name].dtype)
    return out
```

```python
from contextlib import ExitStack

import numpy as np

import concourse.bass as bass
from concourse import mybir

F32 = mybir.dt.float32
F32R = mybir.dt.float32r
I32 = mybir.dt.int32
ALU = mybir.AluOpType
ACT = mybir.ActivationFunctionType
AX_X = mybir.AxisListType.X

P = 128
QUAD = 4
RSQRT_SEED = float(0x5F3759DF)
MASKED = -1.0e37
START = 1


def rope_tables(n, dim, window):
    half = np.arange(0, dim, 2, dtype=np.float32)
    inv_freq = (np.float32(1.0) / np.power(np.float32(10000.0), half / np.float32(dim))).astype(np.float32)
    t = np.arange(n, dtype=np.float32)
    freqs = t[:, None] * inv_freq[None, :]
    base = (half + np.float32(0.4 * dim)) / np.float32(1.4 * dim)
    power = (t - np.float32(n // 2)) / np.float32(window // 2)
    scale = np.power(base[None, :], power[:, None]).astype(np.float32)
    cos, sin = np.cos(freqs), np.sin(freqs)
    two = lambda a, b: np.concatenate([a, b], axis=-1)
    out = np.stack([two(cos * scale, cos * scale), two(-sin * scale, sin * scale),
                    two(cos / scale, cos / scale), two(-sin / scale, sin / scale)], axis=1)
    return out.astype(np.float32)


def band_masks():
    i = np.arange(P)[:, None]
    j = np.arange(3 * P)[None, :] - 2 * P
    seen = (j <= i) & (j >= i - 2 * P)
    rows = [np.where(seen & (j >= lowest), 0.0, MASKED) for lowest in (0, -P, -2 * P)]
    return np.stack(rows, axis=1).astype(np.float32)


def adaln_ffn_program(nc, x, cond, wqT, bq, wk, bk, wvT, bv, woT, bo,
                      wqkv, q_scale, k_scale, wo, ln_g, ln_b, w1, b1, w2, b2, out):
    B, N, D = x.shape
    L, _, QKV = wqkv.shape
    HD = q_scale.shape[1]
    INNER = QKV // 3
    H = INNER // HD
    HID = w2.shape[1]
    CH = 16
    CHD = D // CH
    KT_ = D // P
    PAIRS = INNER // P
    TB = N // P
    TILES = B * TB
    BLOCKS = TILES // QUAD
    BPB = TB // QUAD
    HM = -(-HID // P)
    ROWS = [min(P, HID - m * P) for m in range(HM)]
    WIN = 3
    SLOTS = QUAD + WIN - 1
    HALF = D // 2
    BROWS = N + 1
    SROWS = B * BROWS + QUAD * P + 1
    CW = HALF + CH // 2
    assert HD * 2 == P and D == 4 * P and INNER == 4 * P and TB % QUAD == 0 and CHD * CH == D

    ident_dram = nc.inline_tensor(np.eye(P, dtype=np.float32), "identity_const").ap()
    rope = rope_tables(N, HD, 256).reshape(TB, P, 4, HD).transpose(1, 0, 2, 3)
    rope_dram = nc.inline_tensor(np.ascontiguousarray(rope).reshape(P, TB * 4 * HD), "rope_const").ap()
    mask_dram = nc.inline_tensor(band_masks().reshape(P, 3 * WIN * P), "mask_const").ap()
    head_of = (np.arange(D).reshape(KT_, P).T[:, :, None] // CHD == np.arange(CH)[None, None, :])
    headmask_dram = nc.inline_tensor(
        np.ascontiguousarray((head_of / np.sqrt(CHD)).astype(np.float32)).reshape(P, KT_ * CH), "headmask_const").ap()
    x_in = nc.dram_tensor("x_layer_in", (SROWS, D), F32).ap()
    x_mid = nc.dram_tensor("x_after_attention", (SROWS, D), F32).ap()
    x_rows = x.rearrange("b n d -> (b n) d")
    out_rows = out.rearrange("b n d -> (b n) d")

    ctx = ExitStack()

    sems = []

    def sem(name):
        sems.append(ctx.enter_context(nc.semaphore(name)))
        return sems[-1]

    def sb_in(stack):
        return lambda name, shape, dt=F32: stack.enter_context(nc.sbuf_tensor(name, shape, dt))

    def pair(sb, name, shape):
        return sb(name + "_hi", shape, F32R), sb(name + "_lo", shape, F32R)

    with ctx:
        sb = sb_in(ctx)
        ident = sb("ident", [P, P])
        zero = sb("zero", [P, D])
        f_last_cell = sb("f_last_cell", [P, 1])
        bank = [ctx.enter_context(nc.psum_tensor(f"bank{i}", [P, 512], F32)) for i in range(8)]

        with ExitStack() as st:
            s = sb_in(st)
            c_wv = pair(s, "c_wv", [P, KT_, 2, CW])
            c_wo = pair(s, "c_wo", [P, KT_, D])
            c_wq = s("c_wq", [P, KT_, D])
            c_wk = s("c_wk", [P, KT_, D])
            c_wv_raw = s("c_wv_raw", [P, KT_, D])
            c_wo_raw = s("c_wo_raw", [P, KT_, D])
            c_cond = s("c_cond", [P, KT_, B])
            c_bq = s("c_bq", [P, KT_])
            c_bk = s("c_bk", [P, KT_])
            c_bk_wide = s("c_bk_wide", [P, KT_, P])
            c_headmask = s("c_headmask", [P, KT_, CH])
            c_bv = s("c_bv", [P, D])
            c_bo = s("c_bo", [P, D])
            c_qT = s("c_qT", [P, KT_, B])
            c_qblk = s("c_qblk", [P, KT_, B, CH])
            c_A = s("c_A", [P, KT_, B * CH])
            c_c = s("c_c", [P, B * CH])
            c_x = s("c_x", [P, QUAD, D])
            c_xT = pair(s, "c_xT", [P, 2, KT_, P])
            c_att = s("c_att", [P, 2, CH])
            c_tmp = s("c_tmp", [P, 2, D])
            c_ctx = s("c_ctx", [P, 2, D])
            c_ctxT = pair(s, "c_ctxT", [P, 2, KT_, P])
            c_out = s("c_out", [P, 2, D])

        with ExitStack() as st:
            s = sb_in(st)
            a_w = [pair(s, f"a_w{n}", [P, KT_, 512]) for n in ("q", "k", "v", "o")]
            a_KT = pair(s, "a_KT", [P, PAIRS, SLOTS * P])
            a_V = pair(s, "a_V", [P, SLOTS, INNER])
            a_rope = s("a_rope", [P, TB, 4, HD])
            a_QT = pair(s, "a_QT", [P, 2, PAIRS, P])
            a_hT = pair(s, "a_hT", [P, 2, KT_, P])
            a_h = s("a_h", [P, QUAD, D])
            a_res = s("a_res", [P, 2, D])
            a_out = s("a_out", [P, 2, D])
            a_masks = s("a_masks", [P, 3, WIN * P])
            a_mask = s("a_mask", [P, 2, WIN * P])
            a_OT = pair(s, "a_OT", [P, 2, PAIRS, P])
            a_qk_scale = s("a_qk_scale", [P, 4, HD])
            a_ss = s("a_ss", [P, 2 * H])
            a_rs = s("a_rs", [P, 2 * H])
            a_rt = s("a_rt", [P, 2 * H])
            a_q8 = s("a_q8", [P, 2, 2, H])
            a_max = s("a_max", [P, 2])
            a_bias = s("a_bias", [P, 2])
            a_sum = s("a_sum", [P, 2])
            a_inv = s("a_inv", [P, 2])
            with ExitStack() as st2:
                a_stage = [sb_in(st2)(f"a_stage{i}", [P, KT_, 512]) for i in range(2)]
            a_qraw = s("a_qraw", [P, INNER])
            a_sq = s("a_sq", [P, 2, INNER])
            a_qrot = s("a_qrot", [P, INNER])
            a_kn = s("a_kn", [P, INNER])
            a_krot = s("a_krot", [P, INNER])
            a_tmp = s("a_tmp", [P, INNER])
            a_S = s("a_S", [P, 2, WIN * P])
            a_P = s("a_P", [P, 2, WIN * P])
            a_PT = pair(s, "a_PT", [P, 2, WIN * P])

        with ExitStack() as st:
            s = sb_in(st)
            f_w1 = pair(s, "f_w1", [P, KT_, 2 * HID])
            f_w2 = pair(s, "f_w2", [P, HM, D])
            f_h = s("f_h", [P, QUAD, D])
            f_hraw = s("f_hraw", [P, 2, QUAD * P])
            f_hT = pair(s, "f_hT", [P, KT_, QUAD * P])
            f_res = s("f_res", [P, 2, D])
            f_x = s("f_x", [P, 2, D])
            f_gate = s("f_gate", [P, 2, QUAD * P])
            f_uraw = s("f_uraw", [P, 2, QUAD * P])
            f_u = pair(s, "f_u", [P, 2, QUAD * P])
            f_out = s("f_out", [P, 2, D])
            f_stage1 = s("f_stage1", [P, 2, 2, KT_, P])
            f_stage2 = s("f_stage2", [P, 2, D])
            f_b2 = s("f_b2", [P, D])
            f_b1 = s("f_b1", [P, 2, HM])
            f_ln = s("f_ln", [P, 2, KT_])
            f_stats = s("f_stats", [P, QUAD, 6])
            f_mv = s("f_mv", [P, QUAD, 2])
            f_rs = s("f_rs", [P, 3, QUAD])


        started = ctx.enter_context(nc.semaphore("started"))
        waits_over = {eng.engine: sem(f"waits_over{i}") for i, eng in enumerate((nc.sync, nc.tensor, nc.vector, nc.gpsimd))}
        ident_in = sem("ident_in"); zero_set = sem("zero_set"); pads_out = sem("pads_out")
        c_small_in = sem("c_small_in"); c_wq_in = sem("c_wq_in"); c_wk_in = sem("c_wk_in")
        c_wv_in = sem("c_wv_in"); c_wo_in = sem("c_wo_in"); c_x_in = [sem(f"c_x_in{i}") for i in range(QUAD)]
        c_bk_set = sem("c_bk_set"); c_q_mm = sem("c_q_mm"); c_q_set = sem("c_q_set"); c_A_mm = sem("c_A_mm")
        c_A_set = sem("c_A_set"); c_wvo_hi = sem("c_wvo_hi"); c_wvo_lo = sem("c_wvo_lo"); c_Ab_hi = sem("c_Ab_hi")
        c_Ab_lo = sem("c_Ab_lo"); c_xT_mm = sem("c_xT_mm"); c_xT_hi = sem("c_xT_hi"); c_xT_lo = sem("c_xT_lo")
        c_v_mm = sem("c_v_mm"); c_att_add = sem("c_att_add"); c_att_set = sem("c_att_set"); c_v_biased = sem("c_v_biased")
        c_ctx_set = sem("c_ctx_set"); c_ctxT_mm = sem("c_ctxT_mm"); c_ctxT_hi = sem("c_ctxT_hi")
        c_ctxT_lo = sem("c_ctxT_lo"); c_o_mm = sem("c_o_mm"); c_o_set = sem("c_o_set")
        c_stored = [sem(f"c_stored{i}") for i in range(2)]
        a_const_in = sem("a_const_in"); a_scale_in = sem("a_scale_in"); a_rope_in = sem("a_rope_in")
        a_stage_in = [sem(f"a_stage_in{i}") for i in range(2)]
        a_w_hi = sem("a_w_hi"); a_w_lo = sem("a_w_lo"); a_rope_set = sem("a_rope_set"); a_carry_zero = sem("a_carry_zero")
        a_h_in = [sem(f"a_h_in{i}") for i in range(QUAD)]; a_res_in = [sem(f"a_res_in{i}") for i in range(2)]
        a_hT_mm = sem("a_hT_mm"); a_hT_hi = sem("a_hT_hi"); a_hT_lo = sem("a_hT_lo")
        a_q_mm = sem("a_q_mm"); a_k_mm = sem("a_k_mm"); a_v_mm = sem("a_v_mm")
        a_q_copied = sem("a_q_copied"); a_squared = sem("a_squared"); a_ss_set = sem("a_ss_set")
        a_rs_step = sem("a_rs_step"); a_norms_set = sem("a_norms_set"); a_k_normed = sem("a_k_normed")
        a_rot_step = sem("a_rot_step"); a_q_rotated = sem("a_q_rotated"); a_k_rotated = sem("a_k_rotated")
        a_QT_mm = sem("a_QT_mm"); a_QT_hi = sem("a_QT_hi"); a_QT_lo = sem("a_QT_lo")
        a_KT_mm = sem("a_KT_mm"); a_KT_hi = sem("a_KT_hi"); a_KT_lo = sem("a_KT_lo")
        a_V_hi = sem("a_V_hi"); a_V_lo = sem("a_V_lo"); a_carried = sem("a_carried"); a_mask_set = sem("a_mask_set")
        a_S_mm = sem("a_S_mm"); a_S_masked = sem("a_S_masked"); a_bias_set = sem("a_bias_set")
        a_exp = sem("a_exp"); a_inv_set = sem("a_inv_set"); a_P_set = sem("a_P_set")
        a_PT_mm = sem("a_PT_mm"); a_PT_hi = sem("a_PT_hi"); a_PT_lo = sem("a_PT_lo")
        a_O_mm = sem("a_O_mm"); a_O_hi = sem("a_O_hi"); a_O_lo = sem("a_O_lo")
        a_wo_mm = sem("a_wo_mm"); a_out_set = sem("a_out_set"); a_stored = [sem(f"a_stored{i}") for i in range(2)]
        f_small_in = sem("f_small_in"); f_stage1_in = [sem(f"f_stage1_in{i}") for i in range(2)]
        f_stage2_in = [sem(f"f_stage2_in{i}") for i in range(2)]
        f_w1_step = sem("f_w1_step"); f_w1_hi = sem("f_w1_hi"); f_w1_lo = sem("f_w1_lo"); f_w2_hi = sem("f_w2_hi"); f_w2_lo = sem("f_w2_lo")
        f_h_in = sem("f_h_in"); f_res_in = [sem(f"f_res_in{i}") for i in range(2)]
        f_ln_step = sem("f_ln_step"); f_h_normed = sem("f_h_normed")
        f_hT_mm = sem("f_hT_mm"); f_hT_raw = sem("f_hT_raw"); f_hT_hi = sem("f_hT_hi"); f_hT_lo = sem("f_hT_lo")
        f_a_mm = sem("f_a_mm"); f_g_mm = sem("f_g_mm"); f_gelu = sem("f_gelu"); f_u_raw = sem("f_u_raw")
        f_u_hi = sem("f_u_hi"); f_u_lo = sem("f_u_lo"); f_w2_mm = sem("f_w2_mm"); f_res_step = sem("f_res_step")
        f_out_set = sem("f_out_set"); f_stored = [sem(f"f_stored{i}") for i in range(2)]
        f_last_set = sem("f_last_set")

        PREPS = TILES + 1
        HTS = TILES + 2
        FHTS = (BLOCKS + 1) * KT_

        def row_of(block, tile):
            return (block * QUAD + tile) * P + block // BPB

        def load_shifted(sp, src, dst, row, done):
            sp.dma_start(dst[:, 0:HALF], src[bass.ds(row + 1, P), 0:HALF]).then_inc(done, 16)
            sp.dma_start(dst[:, HALF:D], src[bass.ds(row, P), HALF:D]).then_inc(done, 16)

        def waits_end(eng):
            eng.sem_inc(waits_over[eng.engine], 1)

        def three_passes(pe, dst, w, m, start, stop):
            pe.matmul(dst, w[0], m[0], start=start, stop=False)
            pe.matmul(dst, w[0], m[1], start=False, stop=False)
            return pe.matmul(dst, w[1], m[0], start=False, stop=stop)

        ctx.enter_context(nc.allow_non_contiguous_dma(reason="small vectors laid along the partitions"))
        block = ctx.enter_context(nc.Block())

        @block.sync
        def _(sp):
            def condition():
                sp.dma_start(ident[:], ident_dram).then_inc(ident_in, 16)
                for r in range(QUAD):
                    for i in range(1):
                        sp.dma_start(c_x[:, r, :], x_rows[r * P:(r + 1) * P, :]).then_inc(c_x_in[r], 16)
                sp.dma_start(c_wq[:], wqT.rearrange("(k p) n -> p k n", p=P)).then_inc(c_wq_in, 16)
                sp.dma_start(c_cond[:], cond).then_inc(c_small_in, 16)
                sp.dma_start(c_bq[:], bq.rearrange("(k p) -> p k", p=P)).then_inc(c_small_in, 16)
                sp.dma_start(c_bk[:], bk.rearrange("(k p) -> p k", p=P)).then_inc(c_small_in, 16)
                sp.dma_start(c_headmask[:], headmask_dram.rearrange("p (k h) -> p k h", k=KT_)).then_inc(c_small_in, 16)
                sp.dma_start(c_wk[:], wk.rearrange("(k p) n -> p k n", p=P)).then_inc(c_wk_in, 16)
                sp.dma_start(c_wv_raw[:], wvT.rearrange("(k p) n -> p k n", p=P)).then_inc(c_wv_in, 16)
                sp.dma_start(c_bv[:], bv.unsqueeze(0).to_broadcast([P, D])).then_inc(c_small_in, 16)
                sp.dma_start(c_bo[:], bo.unsqueeze(0).to_broadcast([P, D])).then_inc(c_small_in, 16)
                sp.dma_start(c_wo_raw[:], woT.rearrange("(k p) n -> p k n", p=P)).then_inc(c_wo_in, 16)
                sp.wait_ge(zero_set, START + 1)
                for scratch in (x_in, x_mid):
                    for b in range(B):
                        sp.dma_start(scratch[b * BROWS:b * BROWS + 1, :], zero[0:1, :]).then_inc(pads_out, 16)
                    for r in range(QUAD):
                        sp.dma_start(scratch[B * BROWS + r * P:B * BROWS + (r + 1) * P, :], zero[:]).then_inc(pads_out, 16)
                    sp.dma_start(scratch[SROWS - 1:SROWS, :], zero[0:1, :]).then_inc(pads_out, 16)
                for b in range(B):
                    with sp.Fori(0, BPB) as blk:
                        tile0 = (b * BPB + blk) * QUAD
                        for j in range(QUAD):
                            if True:
                                sp.wait_ge(c_o_set, START + tile0 + j + 1)
                                sp.dma_start(x_in[bass.ds(b * BROWS + 1 + (blk * QUAD + j) * P, P), :],
                                             c_out[:, j % 2, :]).then_inc(c_stored[j % 2], 16)
                            nxt = (b * BPB + blk + 1) if b + 1 < B else (b * BPB) + (blk + 1) % BPB
                            sp.wait_ge(c_xT_mm, START + tile0 + j + 1)
                            sp.dma_start(c_x[:, j, :], x_rows[bass.ds((nxt * QUAD + j) * P, P), :])\
                              .then_inc(c_x_in[j], 16)
                for i in range(2):
                    sp.wait_ge(c_stored[i], START + TILES // 2 * 16)
                for j in range(QUAD):
                    sp.wait_ge(c_x_in[j], START + (BLOCKS + 1) * 16)
                sp.wait_ge(pads_out, START + 16 * 2 * (B + QUAD + 1))

            def attention(l):
                for i in range(2):
                    sp.wait_ge(f_stored[i], START + l * (TILES // 2 * 32))
                    waits_end(sp)
                sp.wait_ge(f_hT_lo, START + l * FHTS)
                sp.wait_ge(f_hT_hi, START + l * FHTS)
                waits_end(sp)
                for j in range(QUAD):
                    load_shifted(sp, x_in, a_h[:, j, :], row_of(0, j), a_h_in[j])
                for c in range(4):
                    src = wqkv[bass.ds(l, 1), :, c * INNER:(c + 1) * INNER] if c < 3 else wo[bass.ds(l, 1), :, :]
                    if c >= 2:
                        sp.wait_ge(a_w_hi, START + 4 * l + c - 1)
                        sp.wait_ge(a_w_lo, START + 4 * l + c - 1)
                    sp.dma_start(a_stage[c % 2][:], src.rearrange("a (k p) n -> p (a k) n", p=P))\
                      .then_inc(a_stage_in[c % 2], 16)
                    if c == 0:
                        sp.dma_start(a_rope[:], rope_dram.rearrange("p (t c d) -> p t c d", t=TB, c=4)).then_inc(a_rope_in, 16)
                        sp.dma_start(a_masks[:], mask_dram.rearrange("p (v n) -> p v n", v=3)).then_inc(a_const_in, 16)
                        for w, v in ((0, q_scale), (2, k_scale)):
                            row = v[bass.ds(l, 1), :]
                            sp.dma_start(a_qk_scale[:, w, :], row.to_broadcast([P, HD])).then_inc(a_scale_in, 16)
                            sp.dma_start(a_qk_scale[:, w + 1, 0:HD // 2],
                                         row[:, HD // 2:HD].to_broadcast([P, HD // 2])).then_inc(a_scale_in, 16)
                            sp.dma_start(a_qk_scale[:, w + 1, HD // 2:HD],
                                         row[:, 0:HD // 2].to_broadcast([P, HD // 2])).then_inc(a_scale_in, 16)
                sp.dma_start(a_res[:, 0, :], x_in[1:1 + P, :]).then_inc(a_res_in[0], 16)
                with sp.Fori(0, BLOCKS) as blk:
                    for j in range(QUAD):
                        tile = l * TILES + blk * QUAD + j
                        sp.wait_ge(a_hT_mm, START + l * HTS + blk * QUAD + j + 1)
                        load_shifted(sp, x_in, a_h[:, j, :], row_of(blk + 1, j), a_h_in[j])
                        sp.wait_ge(a_out_set, START + tile)
                        nxt = row_of(blk, j + 1) if j < QUAD - 1 else row_of(blk + 1, 0)
                        sp.dma_start(a_res[:, (j + 1) % 2, :], x_in[bass.ds(nxt + 1, P), :])\
                          .then_inc(a_res_in[(j + 1) % 2], 16)
                        if j == QUAD - 1:
                            sp.wait_ge(a_KT_hi, START + l * PREPS + blk * QUAD + j + 1)
                            sp.wait_ge(a_KT_lo, START + l * PREPS + blk * QUAD + j + 1)
                            sp.wait_ge(a_V_hi, START + l * PREPS + blk * QUAD + j + 1)
                            sp.wait_ge(a_V_lo, START + l * PREPS + blk * QUAD + j + 1)
                            waits_end(sp)
                            sp.wait_ge(a_O_mm, START + tile * H)
                            for part in range(2):
                                keys, values = a_KT[part][:].bitcast(F32), a_V[part][:].bitcast(F32)
                                sp.dma_start(keys[:, :, 0:2 * P], keys[:, :, QUAD * P:SLOTS * P]).then_inc(a_carried, 16)
                                sp.dma_start(values[:, 0:2, :], values[:, QUAD:SLOTS, :]).then_inc(a_carried, 16)
                        sp.wait_ge(a_out_set, START + tile + 1)
                        sp.dma_start(x_mid[bass.ds(row_of(blk, j) + 1, P), :], a_out[:, j % 2, :])\
                          .then_inc(a_stored[j % 2], 16)

            def feed(l):
                for i in range(2):
                    sp.wait_ge(a_stored[i], START + (l + 1) * (TILES // 2 * 16))
                    waits_end(sp)
                    sp.wait_ge(a_res_in[i], START + ((l + 1) * (TILES // 2 * 16 + (16 if i == 0 else 0))))
                    waits_end(sp)
                for j in range(QUAD):
                    sp.wait_ge(a_h_in[j], START + (l + 1) * ((BLOCKS + 1) * 32))
                waits_end(sp)
                sp.wait_ge(a_carried, START + (l + 1) * (BLOCKS * 64))
                waits_end(sp)
                for done in (a_KT_hi, a_KT_lo, a_V_hi, a_V_lo, a_QT_hi, a_QT_lo):
                    sp.wait_ge(done, START + (l + 1) * PREPS)
                waits_end(sp)
                for done in (a_hT_hi, a_hT_lo):
                    sp.wait_ge(done, START + (l + 1) * HTS)
                waits_end(sp)
                sp.wait_ge(a_mask_set, START + (l + 1) * (2 * (BLOCKS + 1)))
                waits_end(sp)
                for j in range(QUAD):
                    load_shifted(sp, x_mid, f_h[:, j, :], row_of(0, j), f_h_in)
                for w, v in ((0, ln_g), (1, ln_b)):
                    sp.dma_start(f_ln[:, w, :], v[bass.ds(l, 1), :].rearrange("a (k p) -> p (a k)", p=P)).then_inc(f_small_in, 16)
                for m in range(HM):
                    if m >= 2:
                        sp.wait_ge(f_w1_hi, START + HM * l + m - 1)
                        sp.wait_ge(f_w1_lo, START + HM * l + m - 1)
                        sp.wait_ge(f_w2_hi, START + HM * l + m - 1)
                        sp.wait_ge(f_w2_lo, START + HM * l + m - 1)
                    for side in range(2):
                        c0 = side * HID + m * P
                        sp.dma_start(f_stage1[:, m % 2, side, :, 0:ROWS[m]],
                                     w1[bass.ds(l, 1), :, c0:c0 + ROWS[m]].rearrange("a (k p) n -> p (a k) n", p=P))\
                          .then_inc(f_stage1_in[m % 2], 16)
                    sp.dma_start(f_stage2[0:ROWS[m], m % 2, :],
                                 w2[bass.ds(l, 1), m * P:m * P + ROWS[m], :].rearrange("a p n -> (a p) n"))\
                      .then_inc(f_stage2_in[m % 2], 16)
                    if m == 0:
                        for side in range(2):
                            c0 = side * HID
                            sp.dma_start(f_b1[:, side, 0:HM - 1],
                                         b1[bass.ds(l, 1), c0:c0 + (HM - 1) * P].rearrange("a (m p) -> p (a m)", p=P))\
                              .then_inc(f_small_in, 16)
                            sp.dma_start(f_b1[0:ROWS[-1], side, HM - 1:HM],
                                         b1[bass.ds(l, 1), c0 + (HM - 1) * P:c0 + HID].rearrange("a p -> p a"))\
                              .then_inc(f_small_in, 16)
                        sp.dma_start(f_b2[:], b2[bass.ds(l, 1), :].to_broadcast([P, D])).then_inc(f_small_in, 16)
                with sp.Fori(0, BLOCKS) as blk:
                    n = l * BLOCKS + blk
                    sp.wait_ge(f_hT_mm, START + l * FHTS + blk * KT_ + KT_)
                    for j in range(QUAD):
                        load_shifted(sp, x_mid, f_h[:, j, :], row_of(blk + 1, j), f_h_in)
                    for j in range(QUAD):
                        if j >= 2:
                            sp.wait_ge(f_out_set, START + n * QUAD + j - 1)
                        sp.dma_start(f_res[:, j % 2, :], x_mid[bass.ds(row_of(blk, j) + 1, P), :])\
                          .then_inc(f_res_in[j % 2], 16)
                        sp.dma_start(f_x[:, j % 2, :], x_rows[bass.ds((blk * QUAD + j) * P, P), :])\
                          .then_inc(f_res_in[j % 2], 16)
                        if j >= 2:
                            store(l, blk, n, j - 2)
                    for j in range(2, QUAD):
                        store(l, blk, n, j)

            def store(l, blk, n, j):
                sp.wait_ge(f_out_set, START + n * QUAD + j + 1)
                sp.dma_start(x_in[bass.ds(row_of(blk, j) + 1, P), :], f_out[:, j % 2, :]).then_inc(f_stored[j % 2], 16)
                sp.dma_start(out_rows[bass.ds((blk * QUAD + j) * P, P), :], f_out[:, j % 2, :])\
                  .then_inc(f_stored[j % 2], 16)

            sp.wait_ge(started, 1)
            condition()
            with sp.Fori(0, L) as l:
                attention(l)
                feed(l)
            for i in range(2):
                sp.wait_ge(f_stored[i], START + L * (TILES // 2 * 32))
            sp.wait_ge(f_h_in, START + L * (BLOCKS + 1) * QUAD * 32)

        @block.tensor
        def _(pe):
            def transpose_tile(dst, src):
                for k in range(KT_):
                    mm = pe.transpose(dst[:, k * P:(k + 1) * P], src[:, k * P:(k + 1) * P], ident[:])
                return mm

            def condition():
                pe.wait_ge(ident_in, START + 16)
                pe.wait_ge(c_small_in, START + 6 * 16)
                pe.wait_ge(c_wq_in, START + 16)
                for m in range(KT_):
                    for k in range(KT_):
                        mm = pe.matmul(bank[0][:, m * B:(m + 1) * B], c_wq[:, k, m * P:(m + 1) * P], c_cond[:, k, :],
                                       start=(k == 0), stop=(k == KT_ - 1))
                mm.then_inc(c_q_mm, 1)
                pe.wait_ge(c_q_set, START + 2)
                pe.wait_ge(c_wk_in, START + 16)
                pe.wait_ge(c_bk_set, START + 1)
                for k in range(KT_):
                    for m in range(KT_):
                        mm = pe.matmul(bank[1][:, k * B * CH:(k + 1) * B * CH], c_wk[:, m, k * P:(k + 1) * P],
                                       c_qblk[:, m, :, :].rearrange("p b h -> p (b h)"),
                                       start=(m == 0), stop=(m == KT_ - 1))
                for m in range(KT_):
                    mm = pe.matmul(bank[2][:, 0:B * CH], c_bk_wide[:, m, :],
                                   c_qblk[:, m, :, :].rearrange("p b h -> p (b h)"),
                                   start=(m == 0), stop=(m == KT_ - 1))
                mm.then_inc(c_A_mm, 1)
                for b in range(B):
                    with pe.Fori(0, BPB) as blk:
                        t0 = (b * BPB + blk) * QUAD
                        n0 = b * BPB + blk

                        def x_T(j):
                            pe.wait_ge(c_x_in[j], START + (n0 + 1) * 16)
                            pe.wait_ge(c_xT_lo, START + t0 + j)
                            pe.wait_ge(c_xT_hi, START + t0 + j)
                            transpose_tile(bank[0], c_x[:, j, :]).then_inc(c_xT_mm, 1)

                        def v(j):
                            pe.wait_ge(c_xT_hi, START + t0 + j + 1)
                            pe.wait_ge(c_xT_lo, START + t0 + j + 1)
                            if j < 2:
                                pe.wait_ge(c_ctx_set, START + 2 * t0)
                            else:
                                pe.wait_ge(c_ctx_set, START + 2 * (t0 + j - 1))
                            for half in range(2):
                                for k in range(KT_):
                                    mm = three_passes(pe, bank[2 + 2 * (j % 2) + half][:, 0:CW],
                                                      [c_xT[i][:, j % 2, k, :] for i in range(2)],
                                                      [c_wv[i][:, k, half, :] for i in range(2)],
                                                      k == 0, k == KT_ - 1)
                                mm.then_inc(c_v_mm, 1)

                        def ctx_T(j):
                            pe.wait_ge(c_ctx_set, START + 2 * (t0 + j + 1))
                            pe.wait_ge(c_ctxT_lo, START + t0 + j)
                            pe.wait_ge(c_ctxT_hi, START + t0 + j)
                            transpose_tile(bank[1], c_ctx[:, j % 2, :]).then_inc(c_ctxT_mm, 1)

                        def o(j):
                            pe.wait_ge(c_ctxT_hi, START + t0 + j + 1)
                            pe.wait_ge(c_ctxT_lo, START + t0 + j + 1)
                            if j < 2:
                                pe.wait_ge(c_o_set, START + t0)
                            else:
                                pe.wait_ge(c_o_set, START + t0 + j - 1)
                            for k in range(KT_):
                                mm = three_passes(pe, bank[6 + j % 2][:],
                                                  [c_ctxT[i][:, j % 2, k, :] for i in range(2)],
                                                  [c_wo[i][:, k, :] for i in range(2)], k == 0, k == KT_ - 1)
                            mm.then_inc(c_o_mm, 1)

                        x_T(0)
                        pe.wait_ge(c_Ab_hi, START + b + 1)
                        pe.wait_ge(c_Ab_lo, START + b + 1)
                        pe.wait_ge(c_wvo_hi, START + 2)
                        pe.wait_ge(c_wvo_lo, START + 2)
                        x_T(1)
                        v(0)
                        x_T(2)
                        v(1)
                        ctx_T(0)
                        x_T(3)
                        v(2)
                        ctx_T(1)
                        o(0)
                        v(3)
                        ctx_T(2)
                        o(1)
                        ctx_T(3)
                        o(2)
                        o(3)

            def attention(l):
                q_bank, k_bank, v_bank, o_bank = 4, 5, 6, 7

                def h_T(slot, loads, count):
                    pe.wait_ge(a_h_in[slot], START + loads * 32)
                    pe.wait_ge(a_hT_hi, START + count)
                    pe.wait_ge(a_hT_lo, START + count)
                    transpose_tile(bank[v_bank], a_h[:, slot, :]).then_inc(a_hT_mm, 1)

                def project(which, k, par, done):
                    mm = three_passes(pe, bank[(q_bank, k_bank, v_bank)[which]][:],
                                      [a_hT[i][:, par, k, :] for i in range(2)],
                                      [a_w[which][i][:, k, :] for i in range(2)], k == 0, k == KT_ - 1)
                    if k == KT_ - 1:
                        mm.then_inc(done, 1)

                def q_T(count):
                    pe.wait_ge(a_q_rotated, START + count + 1)
                    pe.wait_ge(a_squared, START + 2 * count + 1)
                    transpose_tile(bank[q_bank], a_qrot[:]).then_inc(a_QT_mm, 1)

                def k_T(count):
                    pe.wait_ge(a_k_rotated, START + count + 1)
                    transpose_tile(bank[k_bank], a_krot[:]).then_inc(a_KT_mm, 1)

                pe.wait_ge(a_O_hi, START + l * TILES * H)
                h_T(0, (BLOCKS + 1) * l + 1, l * HTS)
                h_T(1, (BLOCKS + 1) * l + 1, l * HTS + 1)
                for which, done in ((0, a_q_mm), (1, a_k_mm), (2, a_v_mm)):
                    pe.wait_ge(a_w_hi, START + 4 * l + which + 1)
                    pe.wait_ge(a_w_lo, START + 4 * l + which + 1)
                    if which == 2:
                        pe.wait_ge(a_hT_hi, START + l * HTS + 2)
                        pe.wait_ge(a_hT_lo, START + l * HTS + 2)
                    for k in range(KT_):
                        project(which, k, 0, done)
                q_T(l * PREPS)
                k_T(l * PREPS)
                pe.wait_ge(a_w_hi, START + 4 * l + 4)
                pe.wait_ge(a_w_lo, START + 4 * l + 4)
                pe.wait_ge(a_carry_zero, START + 4 * l + 4)
                waits_end(pe)
                with pe.Fori(0, BLOCKS) as blk:
                    for j in range(QUAD):
                        tile = l * TILES + blk * QUAD + j
                        prep = l * PREPS + blk * QUAD + j
                        ht = l * HTS + blk * QUAD + j
                        par = j % 2

                        def scores(h):
                            r = slice((h % 2) * HD, (h % 2) * HD + HD)
                            if h >= 2:
                                pe.wait_ge(a_S_masked, START + tile * H + h - 1)
                            three_passes(pe, bank[h % 2][:, 0:WIN * P],
                                         [a_QT[i][r, par, h // 2, :] for i in range(2)],
                                         [a_KT[i][r, h // 2, j * P:(j + WIN) * P] for i in range(2)],
                                         True, True).then_inc(a_S_mm, 1)

                        def p_T(h):
                            pe.wait_ge(a_P_set, START + tile * H + h + 1)
                            if h >= 2:
                                pe.wait_ge(a_PT_hi, START + tile * H + h - 1)
                                pe.wait_ge(a_PT_lo, START + tile * H + h - 1)
                            for kb in range(WIN):
                                mm = pe.transpose(bank[2 + h % 2][:, kb * P:(kb + 1) * P],
                                                  a_P[:, h % 2, kb * P:(kb + 1) * P], ident[:])
                            mm.then_inc(a_PT_mm, 1)

                        def pv(h):
                            pe.wait_ge(a_PT_hi, START + tile * H + h + 1)
                            pe.wait_ge(a_PT_lo, START + tile * H + h + 1)
                            if h >= 2:
                                pe.wait_ge(a_O_hi, START + tile * H + h - 1)
                                pe.wait_ge(a_O_lo, START + tile * H + h - 1)
                            for kb in range(WIN):
                                mm = three_passes(pe, bank[2 + h % 2][0:HD, WIN * P:WIN * P + P],
                                                  [a_V[i][:, j + kb, h * HD:(h + 1) * HD] for i in range(2)],
                                                  [a_PT[i][:, h % 2, kb * P:(kb + 1) * P] for i in range(2)],
                                                  kb == 0, kb == WIN - 1)
                            mm.then_inc(a_O_mm, 1)

                        work = {0: [(0, 0), (0, 1), (0, 2), (0, 3)], 1: [(1, 0), (1, 1)], 2: [(1, 2), (1, 3)],
                                3: [(2, 0)], 4: [(2, 1)], 5: [(2, 2)], 6: [(2, 3)], 7: []}
                        for ready in (a_QT_hi, a_QT_lo, a_KT_hi, a_KT_lo, a_V_hi, a_V_lo):
                            pe.wait_ge(ready, START + prep + 1)
                        if j == 0:
                            pe.wait_ge(a_carried, START + (l * BLOCKS + blk) * 64)
                        pe.wait_ge(a_S_masked, START + tile * H)
                        pe.wait_ge(a_O_hi, START + tile * H)
                        pe.wait_ge(a_O_lo, START + tile * H)
                        scores(0)
                        scores(1)
                        pe.wait_ge(a_hT_hi, START + ht + 2)
                        pe.wait_ge(a_hT_lo, START + ht + 2)
                        for h in range(H):
                            if 1 <= h < H - 1:
                                scores(h + 1)
                            for which, k in work[h]:
                                project(which, k, 1 - par, (a_q_mm, a_k_mm, a_v_mm)[which])
                            if h >= 1:
                                pv(h - 1)
                            if h == H - 1:
                                q_T(prep + 1)
                            p_T(h)
                        k_T(prep + 1)
                        pv(H - 1)
                        pe.wait_ge(a_V_hi, START + prep + 2)
                        pe.wait_ge(a_V_lo, START + prep + 2)
                        slot = (j + 2) % QUAD
                        h_T(slot, (BLOCKS + 1) * l + blk + (j + 2) // QUAD + 1, ht + 2)
                        pe.wait_ge(a_out_set, START + tile)
                        for k in range(PAIRS):
                            if k == PAIRS - 1:
                                pe.wait_ge(a_O_hi, START + tile * H + H)
                                pe.wait_ge(a_O_lo, START + tile * H + H)
                            elif k == 0:
                                pe.wait_ge(a_O_hi, START + tile * H + H - 2)
                                pe.wait_ge(a_O_lo, START + tile * H + H - 2)
                            mm = three_passes(pe, bank[o_bank][:], [a_OT[i][:, par, k, :] for i in range(2)],
                                              [a_w[3][i][:, k, :] for i in range(2)], k == 0, k == PAIRS - 1)
                        mm.then_inc(a_wo_mm, 1)

            def feed(l):
                def h_T(k, dst):
                    for j in range(QUAD):
                        mm = pe.transpose(dst[:, j * P:(j + 1) * P], f_h[:, j, k * P:(k + 1) * P], ident[:])
                    mm.then_inc(f_hT_mm, 1)

                a_bank, g_bank = (4, 6), (5, 7)
                pe.wait_ge(f_h_normed, START + (l * (BLOCKS + 1) + 1) * QUAD)
                for k in range(KT_):
                    h_T(k, bank[4 + k])
                with pe.Fori(0, BLOCKS) as blk:
                    n = l * BLOCKS + blk
                    pe.wait_ge(f_hT_hi, START + l * FHTS + blk * KT_ + KT_)
                    pe.wait_ge(f_hT_lo, START + l * FHTS + blk * KT_ + KT_)

                    def up(m):
                        if m >= 2:
                            pe.wait_ge(f_u_raw, START + n * HM + m - 1)
                        for which, dst, done in ((0, a_bank[m % 2], f_a_mm), (1, g_bank[m % 2], f_g_mm)):
                            pe.wait_ge(f_w1_hi, START + l * HM + m + 1)
                            pe.wait_ge(f_w1_lo, START + l * HM + m + 1)
                            c0 = which * HID + m * P
                            for k in range(KT_):
                                mm = three_passes(pe, bank[dst][0:ROWS[m], :],
                                                  [f_w1[i][:, k, c0:c0 + ROWS[m]] for i in range(2)],
                                                  [f_hT[i][:, k, :] for i in range(2)], k == 0, k == KT_ - 1)
                            mm.then_inc(done, 1)

                    def down(m):
                        pe.wait_ge(f_u_hi, START + n * HM + m + 1)
                        pe.wait_ge(f_u_lo, START + n * HM + m + 1)
                        pe.wait_ge(f_w2_hi, START + l * HM + m + 1)
                        pe.wait_ge(f_w2_lo, START + l * HM + m + 1)
                        for j in range(QUAD):
                            if m == 0:
                                pe.wait_ge(f_out_set, START + n * QUAD)
                            mm = three_passes(pe, bank[j][:],
                                              [f_u[i][0:ROWS[m], m % 2, j * P:(j + 1) * P] for i in range(2)],
                                              [f_w2[i][0:ROWS[m], m, :] for i in range(2)], m == 0, m == HM - 1)
                        mm.then_inc(f_w2_mm, 1)

                    for m in range(HM):
                        up(m)
                        if m >= 1:
                            down(m - 1)
                    pe.wait_ge(f_h_normed, START + (l * (BLOCKS + 1) + blk + 2) * QUAD)
                    first = (HM - 2) % 2
                    h_T(0, bank[a_bank[first]])
                    h_T(1, bank[g_bank[first]])
                    down(HM - 1)
                    h_T(2, bank[a_bank[1 - first]])
                    h_T(3, bank[g_bank[1 - first]])

            pe.wait_ge(started, 1)
            condition()
            with pe.Fori(0, L) as l:
                attention(l)
                feed(l)

        @block.scalar
        def _(act):
            def condition():
                for n, (raw_in, parts) in enumerate(((c_wv_in, None), (c_wo_in, None))):
                    act.wait_ge(raw_in, START + 16)
                    if n == 0:
                        for half in range(2):
                            cp = act.activation(c_wv[0][:, :, half, 0:HALF],
                                                c_wv_raw[:, :, half * HALF:(half + 1) * HALF], ACT.Copy)
                    else:
                        cp = act.activation(c_wo[0][:], c_wo_raw[:], ACT.Copy)
                    cp.then_inc(c_wvo_hi, 1)
                for b in range(B):
                    act.wait_ge(c_A_set, START + 1)
                    if b > 0:
                        act.wait_ge(c_v_mm, START + 2 * b * TB)
                    for half in range(2):
                        cp = act.activation(c_wv[0][:, :, half, HALF:CW],
                                            c_A[:, :, b * CH + half * (CH // 2):b * CH + (half + 1) * (CH // 2)], ACT.Copy)
                    cp.then_inc(c_Ab_hi, 1)
                    with act.Fori(0, BPB) as blk:
                        t0 = (b * BPB + blk) * QUAD

                        def x_T(j):
                            act.wait_ge(c_xT_mm, START + t0 + j + 1)
                            act.wait_ge(c_v_mm, START + (2 * (t0 if j < 2 else t0 + j - 1)))
                            act.activation(c_xT[0][:, j % 2, :, :], bank[0][:].rearrange("p (k n) -> p k n", k=KT_),
                                           ACT.Copy).then_inc(c_xT_hi, 1)

                        def ctx_T(j):
                            act.wait_ge(c_ctxT_mm, START + t0 + j + 1)
                            act.wait_ge(c_o_mm, START + (t0 if j < 2 else t0 + j - 1))
                            act.activation(c_ctxT[0][:, j % 2, :, :], bank[1][:].rearrange("p (k n) -> p k n", k=KT_),
                                           ACT.Copy).then_inc(c_ctxT_hi, 1)

                        x_T(0)
                        x_T(1)
                        x_T(2)
                        ctx_T(0)
                        x_T(3)
                        ctx_T(1)
                        ctx_T(2)
                        ctx_T(3)

            def attention(l):
                def square(which, count):
                    act.wait_ge((a_q_mm, a_k_mm)[which], START + count + 1)
                    act.wait_ge(a_ss_set, START + count)
                    act.activation(a_sq[:, which, :], bank[4 + which][:], ACT.Square).then_inc(a_squared, 1)

                def q_copy(count):
                    act.wait_ge(a_q_mm, START + count + 1)
                    act.wait_ge(a_q_rotated, START + count)
                    act.activation(a_qraw[:], bank[4][:], ACT.Copy).then_inc(a_q_copied, 1)

                def q_T(count, par):
                    act.wait_ge(a_QT_mm, START + count + 1)
                    act.activation(a_QT[0][:, par, :, :], bank[4][:].rearrange("p (c n) -> p c n", c=PAIRS),
                                   ACT.Copy).then_inc(a_QT_hi, 1)

                def k_T(count, slot, used):
                    act.wait_ge(a_KT_mm, START + count + 1)
                    act.wait_ge(a_O_mm, START + used)
                    act.activation(a_KT[0][:, :, slot * P:(slot + 1) * P], bank[5][:].rearrange("p (c n) -> p c n", c=PAIRS),
                                   ACT.Copy).then_inc(a_KT_hi, 1)

                def value(count, slot, used):
                    act.wait_ge(a_v_mm, START + count + 1)
                    act.wait_ge(a_O_mm, START + used)
                    act.activation(a_V[0][:, slot, :], bank[6][:], ACT.Copy).then_inc(a_V_hi, 1)

                def h_T(count, par):
                    act.wait_ge(a_hT_mm, START + count + 1)
                    act.activation(a_hT[0][:, par, :, :], bank[6][:].rearrange("p (k n) -> p k n", k=KT_),
                                   ACT.Copy).then_inc(a_hT_hi, 1)

                h_T(l * HTS, 0)
                h_T(l * HTS + 1, 1)
                for c in range(4):
                    act.wait_ge(a_stage_in[c % 2], START + (2 * l + c // 2 + 1) * 16)
                    act.activation(a_w[c][0][:], a_stage[c % 2][:], ACT.Copy).then_inc(a_w_hi, 1)
                act.wait_ge(a_w_lo, START + 4 * l + 4)
                q_copy(l * PREPS)
                square(0, l * PREPS)
                square(1, l * PREPS)
                value(l * PREPS, WIN - 1, l * TILES * H)
                q_T(l * PREPS, 0)
                k_T(l * PREPS, WIN - 1, l * TILES * H)
                with act.Fori(0, BLOCKS) as blk:
                    for j in range(QUAD):
                        tile = l * TILES + blk * QUAD + j
                        prep = l * PREPS + blk * QUAD + j
                        ht = l * HTS + blk * QUAD + j
                        par = j % 2
                        slot = j + WIN if j < QUAD - 1 else WIN - 1

                        def exp(h):
                            act.wait_ge(a_bias_set, START + tile * H + h + 1)
                            act.wait_ge(a_PT_mm, START + (tile * H + h - 1 if h >= 2 else tile * H))
                            act.activation(a_P[:, h % 2, :], a_S[:, h % 2, :], ACT.Exp, bias=a_bias[:, h % 2:h % 2 + 1],
                                           scale=a_q8[:, par, 0, h:h + 1], accum_out=a_sum[:, h % 2:h % 2 + 1])\
                               .then_inc(a_exp, 1)

                        def p_T(h):
                            act.wait_ge(a_PT_mm, START + tile * H + h + 1)
                            act.wait_ge(a_O_mm, START + (tile * H + h - 1 if h >= 2 else tile * H))
                            act.activation(a_PT[0][:, h % 2, :], bank[2 + h % 2][:, 0:WIN * P], ACT.Copy).then_inc(a_PT_hi, 1)

                        def o_T(h):
                            r = slice((h % 2) * HD, (h % 2) * HD + HD)
                            act.wait_ge(a_O_mm, START + tile * H + h + 1)
                            if h == 0:
                                act.wait_ge(a_wo_mm, START + tile)
                            act.activation(a_OT[0][r, par, h // 2, :], bank[2 + h % 2][0:HD, WIN * P:WIN * P + P],
                                           ACT.Copy).then_inc(a_O_hi, 1)

                        exp(0)
                        exp(1)
                        for h in range(H):
                            if 1 <= h < H - 1:
                                exp(h + 1)
                            if h == 1:
                                q_copy(prep + 1)
                                square(0, prep + 1)
                            if h == 3:
                                square(1, prep + 1)
                            if h >= 1:
                                o_T(h - 1)
                            if h == H - 1:
                                q_T(prep + 1, 1 - par)
                                value(prep + 1, slot, tile * H)
                            p_T(h)
                        k_T(prep + 1, slot, tile * H)
                        o_T(H - 1)
                        h_T(ht + 2, par)

            def feed(l):
                act.wait_ge(f_small_in, START + (l + 1) * (7 * 16))
                for k in range(KT_):
                    act.wait_ge(f_hT_raw, START + l * FHTS + k + 1)
                    act.activation(f_hT[0][:, k, :], f_hraw[:, k % 2, :], ACT.Copy).then_inc(f_hT_hi, 1)
                with act.Fori(0, BLOCKS) as blk:
                    n = l * BLOCKS + blk

                    def h_T(k):
                        act.wait_ge(f_hT_raw, START + l * FHTS + (blk + 1) * KT_ + k + 1)
                        if k == 0:
                            act.wait_ge(f_g_mm, START + (n + 1) * HM)
                        act.activation(f_hT[0][:, k, :], f_hraw[:, k % 2, :], ACT.Copy).then_inc(f_hT_hi, 1)

                    for m in range(HM):
                        act.wait_ge(f_g_mm, START + n * HM + m + 1)
                        act.wait_ge(f_u_raw, START + (n * HM + m - 1 if m >= 2 else n * HM))
                        act.activation(f_gate[0:ROWS[m], m % 2, :], bank[5 + 2 * (m % 2)][0:ROWS[m], :], ACT.Gelu,
                                       bias=f_b1[0:ROWS[m], 1, m:m + 1]).then_inc(f_gelu, 1)
                        act.wait_ge(f_u_raw, START + n * HM + m + 1)
                        act.wait_ge(f_w2_mm, START + (n * HM + m - 1 if m >= 2 else n * HM))
                        act.activation(f_u[0][0:ROWS[m], m % 2, :], f_uraw[0:ROWS[m], m % 2, :], ACT.Copy)\
                           .then_inc(f_u_hi, 1)
                    for k in range(KT_):
                        h_T(k)

            act.wait_ge(started, 1)
            condition()
            with act.Fori(0, L) as l:
                attention(l)
                feed(l)

        @block.vector
        def _(dve):
            def condition():
                dve.memset(zero[:], 0.0).then_inc(zero_set, 1)
                dve.memset(f_last_cell[:], -1.0).then_inc(f_last_set, 1)
                dve.wait_ge(c_small_in, START + 6 * 16)
                dve.tensor_copy(c_bk_wide[:], c_bk[:].unsqueeze(2).to_broadcast([P, KT_, P])).then_inc(c_bk_set, 1)
                dve.wait_ge(c_q_mm, START + 1)
                dve.tensor_tensor(c_qT[:], bank[0][:, 0:KT_ * B].rearrange("p (k b) -> p k b", k=KT_),
                                  c_bq[:].unsqueeze(2).to_broadcast([P, KT_, B]), ALU.add).then_inc(c_q_set, 1)
                dve.wait_ge(c_q_set, START + 1)
                dve.tensor_tensor(c_qblk[:], c_headmask[:].unsqueeze(2).to_broadcast([P, KT_, B, CH]),
                                  c_qT[:].unsqueeze(3).to_broadcast([P, KT_, B, CH]), ALU.mult).then_inc(c_q_set, 1)
                dve.wait_ge(c_A_mm, START + 1)
                dve.tensor_copy(c_A[:], bank[1][:, 0:KT_ * B * CH].rearrange("p (k n) -> p k n", k=KT_))
                dve.tensor_copy(c_c[:], bank[2][:, 0:B * CH]).then_inc(c_A_set, 1)
                for n in range(2):
                    dve.wait_ge(c_wvo_hi, START + n + 1)
                    if n == 0:
                        for half in range(2):
                            lo = dve.tensor_tensor(c_wv[1][:, :, half, 0:HALF], c_wv_raw[:, :, half * HALF:(half + 1) * HALF],
                                                   c_wv[0][:, :, half, 0:HALF], ALU.subtract)
                    else:
                        lo = dve.tensor_tensor(c_wo[1][:], c_wo_raw[:], c_wo[0][:], ALU.subtract)
                    lo.then_inc(c_wvo_lo, 1)
                dve.wait_ge(c_A_set, START + 1)
                for b in range(B):
                    dve.wait_ge(c_Ab_hi, START + b + 1)
                    for half in range(2):
                        lo = dve.tensor_tensor(c_wv[1][:, :, half, HALF:CW],
                                               c_A[:, :, b * CH + half * (CH // 2):b * CH + (half + 1) * (CH // 2)],
                                               c_wv[0][:, :, half, HALF:CW], ALU.subtract)
                    lo.then_inc(c_Ab_lo, 1)
                    with dve.Fori(0, BPB) as blk:
                        t0 = (b * BPB + blk) * QUAD

                        def x_T(j):
                            dve.wait_ge(c_xT_hi, START + t0 + j + 1)
                            dve.tensor_tensor(c_xT[1][:, j % 2, :, :], bank[0][:].rearrange("p (k n) -> p k n", k=KT_),
                                              c_xT[0][:, j % 2, :, :], ALU.subtract).then_inc(c_xT_lo, 1)

                        def context(j):
                            dve.wait_ge(c_v_mm, START + 2 * (t0 + j + 1))
                            par = j % 2
                            vb = [bank[2 + 2 * par], bank[3 + 2 * par]]
                            for half in range(2):
                                hs = slice(half * (CH // 2), (half + 1) * (CH // 2))
                                dve.tensor_tensor(c_att[:, par, hs], vb[half][:, HALF:CW],
                                                  c_c[:, b * CH + half * (CH // 2):b * CH + (half + 1) * (CH // 2)],
                                                  ALU.add).then_inc(c_att_add, 1)
                            for half in range(2):
                                cs = slice(half * HALF, (half + 1) * HALF)
                                dve.tensor_tensor(c_tmp[:, par, cs], vb[half][:, 0:HALF], c_bv[:, cs], ALU.add)\
                                   .then_inc(c_v_biased, 1)
                            dve.wait_ge(c_att_add, START + 2 * (t0 + j + 1))
                            dve.tensor_scalar(c_att[:, par, :], c_att[:, par, :], 0.0, 1.0, ALU.max, ALU.min)\
                               .then_inc(c_att_set, 1)
                            dve.wait_ge(c_v_biased, START + 2 * (t0 + j + 1))
                            dve.wait_ge(c_att_set, START + t0 + j + 1)
                            dve.wait_ge(c_ctxT_mm, START + (t0 if j < 2 else t0 + j - 1))
                            dve.tensor_tensor(c_ctx[:, par, :].rearrange("p (h d) -> p h d", h=CH),
                                              c_tmp[:, par, :].rearrange("p (h d) -> p h d", h=CH),
                                              c_att[:, par, :].unsqueeze(2).to_broadcast([P, CH, CHD]), ALU.mult)\
                               .then_inc(c_ctx_set, 2)

                        def ctx_T(j):
                            dve.wait_ge(c_ctxT_hi, START + t0 + j + 1)
                            dve.tensor_tensor(c_ctxT[1][:, j % 2, :, :], bank[1][:].rearrange("p (k n) -> p k n", k=KT_),
                                              c_ctxT[0][:, j % 2, :, :], ALU.subtract).then_inc(c_ctxT_lo, 1)

                        def o(j):
                            dve.wait_ge(c_o_mm, START + t0 + j + 1)
                            dve.wait_ge(c_stored[j % 2], START + (t0 // 2 + j // 2) * 16)
                            dve.tensor_tensor(c_out[:, j % 2, :], bank[6 + j % 2][:], c_bo[:], ALU.add).then_inc(c_o_set, 1)

                        x_T(0)
                        x_T(1)
                        context(0)
                        x_T(2)
                        context(1)
                        ctx_T(0)
                        x_T(3)
                        context(2)
                        ctx_T(1)
                        o(0)
                        context(3)
                        ctx_T(2)
                        o(1)
                        ctx_T(3)
                        o(2)
                        o(3)

            def attention(l):
                def sums(count):
                    dve.wait_ge(a_squared, START + 2 * (count + 1))
                    dve.wait_ge(a_norms_set, START + count)
                    dve.tensor_reduce(a_ss[:], a_sq[:].rearrange("p c (h d) -> p (c h) d", d=HD), AX_X, ALU.add)\
                       .then_inc(a_ss_set, 1)

                def k_norm(count):
                    dve.wait_ge(a_norms_set, START + count + 1)
                    dve.wait_ge(a_k_rotated, START + count)
                    dve.tensor_tensor(a_kn[:].rearrange("p (h d) -> p h d", h=H), bank[5][:].rearrange("p (h d) -> p h d", h=H),
                                      a_rs[:, H:2 * H].unsqueeze(2).to_broadcast([P, H, HD]), ALU.mult).then_inc(a_k_normed, 1)

                def q_T(count, par):
                    dve.wait_ge(a_QT_hi, START + count + 1)
                    dve.tensor_tensor(a_QT[1][:, par, :, :], bank[4][:].rearrange("p (c n) -> p c n", c=PAIRS),
                                      a_QT[0][:, par, :, :], ALU.subtract).then_inc(a_QT_lo, 1)

                def k_T(count, slot):
                    dve.wait_ge(a_KT_hi, START + count + 1)
                    dve.tensor_tensor(a_KT[1][:, :, slot * P:(slot + 1) * P], bank[5][:].rearrange("p (c n) -> p c n", c=PAIRS),
                                      a_KT[0][:, :, slot * P:(slot + 1) * P], ALU.subtract).then_inc(a_KT_lo, 1)

                def value(count, slot):
                    dve.wait_ge(a_V_hi, START + count + 1)
                    dve.tensor_tensor(a_V[1][:, slot, :], bank[6][:], a_V[0][:, slot, :], ALU.subtract).then_inc(a_V_lo, 1)

                def h_T(count, par):
                    dve.wait_ge(a_hT_hi, START + count + 1)
                    dve.tensor_tensor(a_hT[1][:, par, :, :], bank[6][:].rearrange("p (k n) -> p k n", k=KT_),
                                      a_hT[0][:, par, :, :], ALU.subtract).then_inc(a_hT_lo, 1)

                h_T(l * HTS, 0)
                h_T(l * HTS + 1, 1)
                for c in range(4):
                    dve.wait_ge(a_w_hi, START + 4 * l + c + 1)
                    dve.tensor_tensor(a_w[c][1][:], a_stage[c % 2][:], a_w[c][0][:], ALU.subtract).then_inc(a_w_lo, 1)
                sums(l * PREPS)
                value(l * PREPS, WIN - 1)
                k_norm(l * PREPS)
                q_T(l * PREPS, 0)
                k_T(l * PREPS, WIN - 1)
                with dve.Fori(0, BLOCKS) as blk:
                    for j in range(QUAD):
                        tile = l * TILES + blk * QUAD + j
                        prep = l * PREPS + blk * QUAD + j
                        ht = l * HTS + blk * QUAD + j
                        par = j % 2
                        slot = j + WIN if j < QUAD - 1 else WIN - 1

                        def mask_max(h):
                            b = h % 2
                            dve.wait_ge(a_exp, START + (tile * H + h - 1 if h >= 2 else tile * H))
                            dve.wait_ge(a_S_mm, START + tile * H + h + 1)
                            if j < 2 and h == 0:
                                dve.wait_ge(a_mask_set, START + (l * (BLOCKS + 1) + blk + 1) * 2)
                            dve.wait_ge(a_const_in, START + 16)
                            waits_end(dve)
                            dve.tensor_tensor_reduce(a_S[:, b, :], bank[b][:, 0:WIN * P],
                                                     a_mask[:, j, :] if j < 2 else a_masks[:, 2, :], 1.0, -3.0e38,
                                                     ALU.add, ALU.max, a_max[:, b:b + 1]).then_inc(a_S_masked, 1)
                            dve.wait_ge(a_S_masked, START + tile * H + h + 1)
                            dve.tensor_scalar(a_bias[:, b:b + 1], a_max[:, b:b + 1], a_q8[:, par, 1, h:h + 1], None, ALU.mult)\
                               .then_inc(a_bias_set, 1)

                        def normalize(h):
                            b = h % 2
                            dve.wait_ge(a_exp, START + tile * H + h + 1)
                            dve.reciprocal(a_inv[:, b:b + 1], a_sum[:, b:b + 1]).then_inc(a_inv_set, 1)
                            dve.wait_ge(a_inv_set, START + tile * H + h + 1)
                            dve.tensor_scalar(a_P[:, b, :], a_P[:, b, :], a_inv[:, b:b + 1], None, ALU.mult).then_inc(a_P_set, 1)

                        def p_T(h):
                            dve.wait_ge(a_PT_hi, START + tile * H + h + 1)
                            dve.tensor_tensor(a_PT[1][:, h % 2, :], bank[2 + h % 2][:, 0:WIN * P], a_PT[0][:, h % 2, :],
                                              ALU.subtract).then_inc(a_PT_lo, 1)

                        def o_T(h):
                            r = slice((h % 2) * HD, (h % 2) * HD + HD)
                            dve.wait_ge(a_O_hi, START + tile * H + h + 1)
                            dve.tensor_tensor(a_OT[1][r, par, h // 2, :], bank[2 + h % 2][0:HD, WIN * P:WIN * P + P],
                                              a_OT[0][r, par, h // 2, :], ALU.subtract).then_inc(a_O_lo, 1)

                        dve.wait_ge(a_norms_set, START + prep + 1)
                        mask_max(0)
                        mask_max(1)
                        for h in range(H):
                            normalize(h)
                            if 1 <= h < H - 1:
                                mask_max(h + 1)
                            if h >= 1:
                                o_T(h - 1)
                            if h == 3:
                                sums(prep + 1)
                            if h == 5:
                                k_norm(prep + 1)
                            if h == H - 1:
                                q_T(prep + 1, 1 - par)
                                value(prep + 1, slot)
                            p_T(h)
                        k_T(prep + 1, slot)
                        o_T(H - 1)
                        h_T(ht + 2, par)
                        dve.wait_ge(a_wo_mm, START + tile + 1)
                        dve.wait_ge(a_res_in[j % 2],
                                    START + ((l * (TILES // 2 + (1 if j % 2 == 0 else 0)) + blk * (QUAD // 2) + j // 2 + 1) * 16))
                        dve.wait_ge(a_stored[j % 2], START + (l * (TILES // 2) + blk * (QUAD // 2) + j // 2) * 16)
                        dve.tensor_tensor(a_out[:, j % 2, :], bank[7][:], a_res[:, j % 2, :], ALU.add).then_inc(a_out_set, 1)

            def feed(l):
                LN = 15 + 2 * QUAD

                def step(k, base, ins):
                    ins.then_inc(f_ln_step, 1)
                    dve.wait_ge(f_ln_step, START + base + k + 1)

                def normalize(count):
                    dve.wait_ge(f_h_in, START + (count + 1) * (QUAD * 32))
                    base = count * LN
                    for j in range(QUAD):
                        dve.bn_stats(f_stats[:, j, :], f_h[:, j, :]).then_inc(f_ln_step, 1)
                    dve.wait_ge(f_ln_step, START + base + QUAD)
                    waits_end(dve)
                    for j in range(QUAD):
                        dve.bn_aggr(f_mv[:, j, :], f_stats[:, j, :]).then_inc(f_ln_step, 1)
                    dve.wait_ge(f_ln_step, START + base + 2 * QUAD)
                    k = 2 * QUAD
                    var, y, t = f_rs[:, 0, :], f_rs[:, 1, :], f_rs[:, 2, :]
                    step(k, base, dve.tensor_scalar(var, f_mv[:, :, 1], 1e-5, None, ALU.add))
                    step(k + 1, base, dve.tensor_scalar(y.bitcast(I32), var.bitcast(I32), -0.5, RSQRT_SEED, ALU.mult, ALU.add))
                    for i in range(4):
                        step(k + 2 + 3 * i, base, dve.tensor_tensor(t, y, y, ALU.mult))
                        step(k + 3 + 3 * i, base, dve.scalar_tensor_tensor(t, t, -0.5, var, ALU.mult, ALU.mult))
                        step(k + 4 + 3 * i, base, dve.scalar_tensor_tensor(y, t, 1.5, y, ALU.add, ALU.mult))
                    step(k + 14, base, dve.memset(t, 0.0))
                    for j in range(QUAD):
                        dve.tensor_scalar(f_h[:, j, :], f_h[:, j, :], f_mv[:, j, 0:1], f_rs[:, 1, j:j + 1],
                                          ALU.subtract, ALU.mult).then_inc(f_h_normed, 1)

                def h_T_raw(count, src, k):
                    dve.wait_ge(f_hT_mm, START + count + 1)
                    if k >= 2:
                        dve.wait_ge(f_hT_lo, START + count - 1)
                    dve.tensor_scalar(f_hraw[:, k % 2, :], src[:], f_ln[:, 0, k:k + 1], f_ln[:, 1, k:k + 1],
                                      ALU.mult, ALU.add).then_inc(f_hT_raw, 1)

                def h_T_lo(count, k):
                    dve.wait_ge(f_hT_hi, START + count + 1)
                    dve.tensor_tensor(f_hT[1][:, k, :], f_hraw[:, k % 2, :], f_hT[0][:, k, :], ALU.subtract)\
                       .then_inc(f_hT_lo, 1)

                dve.wait_ge(f_last_set, START + l + 1)
                dve.tensor_scalar(f_last_cell[:], f_last_cell[:], 1.0, None, ALU.add).then_inc(f_last_set, 1)
                dve.wait_ge(f_last_set, START + l + 2)
                dve.wait_ge(f_small_in, START + (l + 1) * (7 * 16))
                normalize(l * (BLOCKS + 1))
                for k in range(KT_):
                    h_T_raw(l * FHTS + k, bank[4 + k], k)
                    h_T_lo(l * FHTS + k, k)
                with dve.Fori(0, BLOCKS) as blk:
                    n = l * BLOCKS + blk
                    nh = l * FHTS + (blk + 1) * KT_

                    def hidden(m):
                        dve.wait_ge(f_gelu, START + n * HM + m + 1)
                        dve.wait_ge(f_a_mm, START + n * HM + m + 1)
                        dve.wait_ge(f_u_hi, START + (n * HM + m - 1 if m >= 2 else n * HM))
                        dve.scalar_tensor_tensor(f_uraw[0:ROWS[m], m % 2, :], bank[4 + 2 * (m % 2)][0:ROWS[m], :],
                                                 f_b1[0:ROWS[m], 0, m:m + 1], f_gate[0:ROWS[m], m % 2, :],
                                                 ALU.add, ALU.mult).then_inc(f_u_raw, 1)
                        dve.wait_ge(f_u_hi, START + n * HM + m + 1)
                        dve.tensor_tensor(f_u[1][0:ROWS[m], m % 2, :], f_uraw[0:ROWS[m], m % 2, :],
                                          f_u[0][0:ROWS[m], m % 2, :], ALU.subtract).then_inc(f_u_lo, 1)

                    def residual(j):
                        s = 2 * (n * QUAD + j)
                        dve.wait_ge(f_res_in[j % 2], START + (n * QUAD // 2 + j // 2 + 1) * 32)
                        dve.scalar_tensor_tensor(f_res[:, j % 2, :], f_x[:, j % 2, :], f_last_cell[:], f_res[:, j % 2, :],
                                                 ALU.mult, ALU.add).then_inc(f_res_step, 1)
                        dve.wait_ge(f_res_step, START + s + 1)
                        dve.tensor_tensor(f_res[:, j % 2, :], f_res[:, j % 2, :], f_b2[:], ALU.add).then_inc(f_res_step, 1)

                    def result(j):
                        dve.wait_ge(f_w2_mm, START + (n + 1) * HM)
                        dve.wait_ge(f_res_step, START + 2 * (n * QUAD + j + 1))
                        dve.wait_ge(f_stored[j % 2], START + (n * QUAD // 2 + j // 2) * 32)
                        dve.tensor_tensor(f_out[:, j % 2, :], bank[j][:], f_res[:, j % 2, :], ALU.add).then_inc(f_out_set, 1)

                    for m in range(HM):
                        hidden(m)
                        if m == 3:
                            normalize(l * (BLOCKS + 1) + blk + 1)
                        if m == 5:
                            residual(0)
                            residual(1)
                    first = (HM - 2) % 2
                    h_T_raw(nh, bank[4 + 2 * first], 0)
                    h_T_raw(nh + 1, bank[5 + 2 * first], 1)
                    h_T_lo(nh, 0)
                    h_T_raw(nh + 2, bank[6 - 2 * first], 2)
                    h_T_lo(nh + 1, 1)
                    h_T_raw(nh + 3, bank[7 - 2 * first], 3)
                    h_T_lo(nh + 2, 2)
                    h_T_lo(nh + 3, 3)
                    result(0)
                    result(1)
                    residual(2)
                    result(2)
                    residual(3)
                    result(3)

            dve.wait_ge(started, 1)
            condition()
            with dve.Fori(0, L) as l:
                attention(l)
                feed(l)

        @block.gpsimd
        def _(pool):
            def attention(l):
                RS = 15
                ROT = 4

                def step(k, base, ins):
                    ins.then_inc(a_rs_step, 1)
                    pool.wait_ge(a_rs_step, START + base + k + 1)

                def norms(count, par):
                    base = count * RS
                    pool.wait_ge(a_ss_set, START + count + 1)
                    pool.wait_ge(a_k_normed, START + count)
                    waits_end(pool)
                    step(0, base, pool.tensor_scalar(a_ss[:], a_ss[:], 1e-24, None, ALU.max))
                    waits_end(pool)
                    step(1, base, pool.tensor_scalar(a_rs[:].bitcast(I32), a_ss[:].bitcast(I32), -0.5, RSQRT_SEED,
                                                     ALU.mult, ALU.add))
                    for i in range(3):
                        step(2 + 4 * i, base, pool.tensor_tensor(a_rt[:], a_rs[:], a_rs[:], ALU.mult))
                        step(3 + 4 * i, base, pool.tensor_tensor(a_rt[:], a_rt[:], a_ss[:], ALU.mult))
                        waits_end(pool)
                        step(4 + 4 * i, base, pool.tensor_scalar(a_rt[:], a_rt[:], -0.5, 1.5, ALU.mult, ALU.add))
                        step(5 + 4 * i, base, pool.tensor_tensor(a_rs[:], a_rs[:], a_rt[:], ALU.mult))
                    waits_end(pool)
                    step(14, base, pool.tensor_scalar(a_q8[:, par, 0, :], a_rs[:, 0:H], 8.0, None, ALU.mult))
                    waits_end(pool)
                    pool.tensor_scalar(a_q8[:, par, 1, :], a_rs[:, 0:H], -8.0, None, ALU.mult).then_inc(a_norms_set, 1)

                def rotate(count, which, src, dst, at, done, used):
                    base = count * ROT + 2 * which
                    halves = lambda a: a.rearrange("p (h t d) -> p h t d", h=H, t=2)
                    table = lambda c: a_rope[:, bass.ds(at, 1), 2 * which + c, :].rearrange("p a (t d) -> p a t d", t=2)\
                        .to_broadcast([P, H, 2, HD // 2])
                    pool.wait_ge(used, START + count)
                    pool.tensor_tensor(halves(a_tmp[:]), halves(src)[:, :, ::-1, :], table(1), ALU.mult).then_inc(a_rot_step, 1)
                    pool.tensor_tensor(halves(dst), halves(src), table(0), ALU.mult).then_inc(a_rot_step, 1)
                    pool.wait_ge(a_rot_step, START + base + 2)
                    pool.tensor_tensor(dst, dst, a_tmp[:], ALU.add).then_inc(done, 1)

                def rotate_q(count, at):
                    pool.wait_ge(a_q_copied, START + count + 1)
                    pool.wait_ge(a_k_rotated, START + count)
                    rotate(count, 0, a_qraw[:], a_qrot[:], at, a_q_rotated, a_QT_mm)

                def rotate_k(count, at):
                    pool.wait_ge(a_k_normed, START + count + 1)
                    pool.wait_ge(a_q_rotated, START + count + 1)
                    rotate(count, 1, a_kn[:], a_krot[:], at, a_k_rotated, a_KT_mm)

                def masks(first):
                    for t in range(2):
                        at = 2 * first if t == 0 else first + 1
                        pool.tensor_copy(a_mask[:, t, :].rearrange("p (a n) -> p a n", a=1),
                                         a_masks[:, bass.ds(at, 1), :]).then_inc(a_mask_set, 1)

                pool.wait_ge(a_scale_in, START + (l + 1) * (6 * 16))
                pool.wait_ge(a_rope_in, START + (l + 1) * 16)
                pool.tensor_tensor(a_rope[:], a_rope[:], a_qk_scale[:].unsqueeze(1).to_broadcast([P, TB, 4, HD]), ALU.mult)\
                    .then_inc(a_rope_set, 1)
                for part in range(2):
                    pool.memset(a_KT[part][:].bitcast(F32)[:, :, 0:2 * P], 0.0).then_inc(a_carry_zero, 1)
                    pool.memset(a_V[part][:].bitcast(F32)[:, 0:2, :], 0.0).then_inc(a_carry_zero, 1)
                pool.wait_ge(a_const_in, START + (l + 1) * 16)
                waits_end(pool)
                masks(0)
                pool.wait_ge(a_rope_set, START + l + 1)
                rotate_q(l * PREPS, 0)
                norms(l * PREPS, 0)
                rotate_k(l * PREPS, 0)
                with pool.Fori(0, BLOCKS) as blk:
                    for j in range(QUAD):
                        tile = l * TILES + blk * QUAD + j
                        prep = l * PREPS + blk * QUAD + j
                        par = j % 2
                        at = (blk % BPB) * QUAD + j + 1 if j < QUAD - 1 else ((blk + 1) % BPB) * QUAD
                        if j == 2:
                            pool.wait_ge(a_S_masked, START + tile * H)
                            masks(((blk + 1) % BPB + BPB - 1) // BPB)
                        rotate_q(prep + 1, at)
                        pool.wait_ge(a_bias_set, START + tile * H)
                        pool.wait_ge(a_exp, START + tile * H)
                        norms(prep + 1, 1 - par)
                        rotate_k(prep + 1, at)

            def feed(l):
                for m in range(HM):
                    pool.wait_ge(f_stage1_in[m % 2], START + (l * ((HM + 1 - m % 2) // 2) + m // 2 + 1) * 32)
                    waits_end(pool)
                    wide = lambda part: f_w1[part][:, :, :].rearrange("p k (s n) -> p s k n", s=2)[:, :, :, m * P:m * P + ROWS[m]]
                    raw = f_stage1[:, m % 2, :, :, 0:ROWS[m]]
                    for side in range(2):
                        pool.tensor_copy(wide(0)[:, side], raw[:, side]).then_inc(f_w1_step, 1)
                    pool.wait_ge(f_w1_step, START + (l * HM + m + 1) * 2)
                    for side in range(2):
                        lo = pool.tensor_tensor(wide(1)[:, side], raw[:, side], wide(0)[:, side], ALU.subtract)
                        if side == 0:
                            lo.then_inc(f_w1_hi, 1)
                        else:
                            lo.then_inc(f_w1_lo, 1)
                    pool.wait_ge(f_stage2_in[m % 2], START + (l * ((HM + 1 - m % 2) // 2) + m // 2 + 1) * 16)
                    waits_end(pool)
                    pool.tensor_copy(f_w2[0][0:ROWS[m], m, :], f_stage2[0:ROWS[m], m % 2, :]).then_inc(f_w2_hi, 1)
                    pool.wait_ge(f_w2_hi, START + l * HM + m + 1)
                    pool.tensor_tensor(f_w2[1][0:ROWS[m], m, :], f_stage2[0:ROWS[m], m % 2, :], f_w2[0][0:ROWS[m], m, :],
                                       ALU.subtract).then_inc(f_w2_lo, 1)

            for s in sems:
                pool.sem_inc(s, START)
            pool.sem_inc(started, 1)
            with pool.Fori(0, L) as l:
                attention(l)
                feed(l)


_INS = ["x", "cond_1024", "L0_cond_Wq", "L0_cond_bq", "L0_cond_Wk", "L0_cond_bk", "L0_cond_Wv", "L0_cond_bv",
        "L0_cond_Wo", "L0_cond_bo", "L0_ffn_wqkv", "L0_ffn_q_scale", "L0_ffn_k_scale", "L0_ffn_wo", "L0_ffn_ln_g",
        "L0_ffn_ln_b", "L0_ffn_w1", "L0_ffn_b1", "L0_ffn_w2", "L0_ffn_b2"]
_TRANSPOSED = ("L0_cond_Wq", "L0_cond_Wv", "L0_cond_Wo")


def kernel(**inputs):
    import concourse.bacc as bacc
    from concourse.bass_utils import run_bass_kernel_spmd

    nc = bacc.Bacc("TRN2", target_bir_lowering=False, num_devices=1)
    arrays, args = {}, []
    for name in _INS:
        a = np.asarray(inputs[name])
        if name == "cond_1024":
            a = a.reshape(a.shape[0], -1, P).transpose(2, 1, 0)
        a = np.ascontiguousarray(a.T if name in _TRANSPOSED else a)
        arrays[f"in_{name}"] = a
        args.append(nc.dram_tensor(f"in_{name}", a.shape, mybir.dt.from_np(a.dtype), kind="ExternalInput").ap())
    shape = tuple(np.asarray(inputs["x"]).shape)
    args.append(nc.dram_tensor("out", shape, F32, kind="ExternalOutput").ap())
    adaln_ffn_program(nc, *args)
    r = run_bass_kernel_spmd(nc, [arrays], core_ids=[0])
    return r.results[0]["out"]
```

```python
from contextlib import ExitStack

import numpy as np

import concourse.bass as bass
from concourse import mybir

F32 = mybir.dt.float32
F32R = mybir.dt.float32r
I32 = mybir.dt.int32
ALU = mybir.AluOpType
ACT = mybir.ActivationFunctionType
AX_X = mybir.AxisListType.X

P = 128
QUAD = 4
RSQRT_SEED = float(0x5F3759DF)
MASKED = -1.0e37
START = 1


def rope_tables(n, dim, window):
    half = np.arange(0, dim, 2, dtype=np.float32)
    inv_freq = (np.float32(1.0) / np.power(np.float32(10000.0), half / np.float32(dim))).astype(np.float32)
    t = np.arange(n, dtype=np.float32)
    freqs = t[:, None] * inv_freq[None, :]
    base = (half + np.float32(0.4 * dim)) / np.float32(1.4 * dim)
    power = (t - np.float32(n // 2)) / np.float32(window // 2)
    scale = np.power(base[None, :], power[:, None]).astype(np.float32)
    cos, sin = np.cos(freqs), np.sin(freqs)
    two = lambda a, b: np.concatenate([a, b], axis=-1)
    out = np.stack([two(cos * scale, cos * scale), two(-sin * scale, sin * scale),
                    two(cos / scale, cos / scale), two(-sin / scale, sin / scale)], axis=1)
    return out.astype(np.float32)


def band_masks():
    i = np.arange(P)[:, None]
    j = np.arange(3 * P)[None, :] - 2 * P
    seen = (j <= i) & (j >= i - 2 * P)
    rows = [np.where(seen & (j >= lowest), 0.0, MASKED) for lowest in (0, -P, -2 * P)]
    return np.stack(rows, axis=1).astype(np.float32)


def adaln_ffn_program(nc, x, cond, wqT, bq, wk, bk, wvT, bv, woT, bo,
                      wqkv, q_scale, k_scale, wo, ln_g, ln_b, w1, b1, w2, b2, out):
    B, N, D = x.shape
    L, _, QKV = wqkv.shape
    HD = q_scale.shape[1]
    INNER = QKV // 3
    H = INNER // HD
    HID = w2.shape[1]
    CH = 16
    CHD = D // CH
    KT_ = D // P
    PAIRS = INNER // P
    TB = N // P
    TILES = B * TB
    BLOCKS = TILES // QUAD
    BPB = TB // QUAD
    HM = -(-HID // P)
    ROWS = [min(P, HID - m * P) for m in range(HM)]
    WIN = 3
    SLOTS = QUAD + WIN - 1
    HALF = D // 2
    BROWS = N + 1
    SROWS = B * BROWS + QUAD * P + 1
    CW = HALF + CH // 2
    assert HD * 2 == P and D == 4 * P and INNER == 4 * P and TB % QUAD == 0 and CHD * CH == D

    ident_dram = nc.inline_tensor(np.eye(P, dtype=np.float32), "identity_const").ap()
    rope = rope_tables(N, HD, 256).reshape(TB, P, 4, HD).transpose(1, 0, 2, 3)
    rope_dram = nc.inline_tensor(np.ascontiguousarray(rope).reshape(P, TB * 4 * HD), "rope_const").ap()
    mask_dram = nc.inline_tensor(band_masks().reshape(P, 3 * WIN * P), "mask_const").ap()
    head_of = (np.arange(D).reshape(KT_, P).T[:, :, None] // CHD == np.arange(CH)[None, None, :])
    headmask_dram = nc.inline_tensor(
        np.ascontiguousarray((head_of / np.sqrt(CHD)).astype(np.float32)).reshape(P, KT_ * CH), "headmask_const").ap()
    x_in = nc.dram_tensor("x_layer_in", (SROWS, D), F32).ap()
    x_mid = nc.dram_tensor("x_after_attention", (SROWS, D), F32).ap()
    x_rows = x.rearrange("b n d -> (b n) d")
    out_rows = out.rearrange("b n d -> (b n) d")

    ctx = ExitStack()

    sems = []

    def sem(name):
        sems.append(ctx.enter_context(nc.semaphore(name)))
        return sems[-1]

    def sb_in(stack):
        return lambda name, shape, dt=F32: stack.enter_context(nc.sbuf_tensor(name, shape, dt))

    def pair(sb, name, shape):
        return sb(name + "_hi", shape, F32R), sb(name + "_lo", shape, F32R)

    with ctx:
        sb = sb_in(ctx)
        ident = sb("ident", [P, P])
        zero = sb("zero", [P, D])
        f_last_cell = sb("f_last_cell", [P, 1])
        out_tiles = sb("out_tiles", [P, 2, D])
        bank = [ctx.enter_context(nc.psum_tensor(f"bank{i}", [P, 512], F32)) for i in range(8)]

        with ExitStack() as st:
            s = sb_in(st)
            c_wv = pair(s, "c_wv", [P, KT_, 2, CW])
            c_wo = pair(s, "c_wo", [P, KT_, D])
            c_wq = s("c_wq", [P, KT_, D])
            c_wk = s("c_wk", [P, KT_, D])
            c_wv_raw = s("c_wv_raw", [P, KT_, D])
            c_wo_raw = s("c_wo_raw", [P, KT_, D])
            c_cond = s("c_cond", [P, KT_, B])
            c_bq = s("c_bq", [P, KT_])
            c_bk = s("c_bk", [P, KT_])
            c_bk_wide = s("c_bk_wide", [P, KT_, P])
            c_headmask = s("c_headmask", [P, KT_, CH])
            c_bv = s("c_bv", [P, D])
            c_bo = s("c_bo", [P, D])
            c_qT = s("c_qT", [P, KT_, B])
            c_qblk = s("c_qblk", [P, KT_, B, CH])
            c_A = s("c_A", [P, KT_, B * CH])
            c_c = s("c_c", [P, B * CH])
            c_x = s("c_x", [P, QUAD, D])
            c_xT = pair(s, "c_xT", [P, 2, KT_, P])
            c_att = s("c_att", [P, 2, CH])
            c_tmp = s("c_tmp", [P, 2, D])
            c_ctx = s("c_ctx", [P, 2, D])
            c_ctxT = pair(s, "c_ctxT", [P, 2, KT_, P])

        with ExitStack() as st:
            s = sb_in(st)
            a_w = [pair(s, f"a_w{n}", [P, KT_, 512]) for n in ("q", "k", "v", "o")]
            a_KT = pair(s, "a_KT", [P, PAIRS, SLOTS * P])
            a_V = pair(s, "a_V", [P, SLOTS, INNER])
            a_rope = s("a_rope", [P, TB, 4, HD])
            a_QT = pair(s, "a_QT", [P, 2, PAIRS, P])
            a_hT = pair(s, "a_hT", [P, 2, KT_, P])
            a_h = s("a_h", [P, QUAD, D])
            a_res = s("a_res", [P, 2, D])
            a_masks = s("a_masks", [P, 3, WIN * P])
            a_mask = s("a_mask", [P, 2, WIN * P])
            a_OT = pair(s, "a_OT", [P, 2, PAIRS, P])
            a_qk_scale = s("a_qk_scale", [P, 4, HD])
            a_ss = s("a_ss", [P, 2 * H])
            a_rs = s("a_rs", [P, 2 * H])
            a_rt = s("a_rt", [P, 2 * H])
            a_q8 = s("a_q8", [P, 2, H])
            a_bias = s("a_bias", [P, 2])
            a_sum = s("a_sum", [P, 3])
            a_inv = s("a_inv", [P, 3])
            with ExitStack() as st2:
                a_stage = [sb_in(st2)(f"a_stage{i}", [P, KT_, 512]) for i in range(2)]
            a_qraw = s("a_qraw", [P, INNER])
            a_sq = s("a_sq", [P, 2, INNER])
            a_qrot = s("a_qrot", [P, INNER])
            a_kn = s("a_kn", [P, INNER])
            a_krot = s("a_krot", [P, INNER])
            a_tmp = s("a_tmp", [P, INNER])
            a_S = s("a_S", [P, 2, WIN * P])
            a_P = s("a_P", [P, 3, WIN * P])
            a_PT = pair(s, "a_PT", [P, 2, WIN * P])

        with ExitStack() as st:
            s = sb_in(st)
            f_h = s("f_h", [P, QUAD, D])
            f_res = s("f_res", [P, 2, D])
            f_x = s("f_x", [P, 2, D])
            f_stage1 = s("f_stage1", [P, 2, 2, KT_, P])
            f_stage2 = s("f_stage2", [P, 2, D])
            f_b2 = s("f_b2", [P, D])
            f_b1 = s("f_b1", [P, 2, HM])
            f_ln = s("f_ln", [P, 2, KT_])
            f_stats = s("f_stats", [P, QUAD, 6])
            f_mv = s("f_mv", [P, QUAD, 2])
            f_rs = s("f_rs", [P, 3, QUAD])
            f_w1 = pair(s, "f_w1", [P, KT_, 2 * HID])
            f_w2 = pair(s, "f_w2", [P, HM, D])
            f_hraw = s("f_hraw", [P, 2, QUAD * P])
            f_hT = pair(s, "f_hT", [P, KT_, QUAD * P])
            f_gate = s("f_gate", [P, 2, QUAD * P])
            f_uraw = s("f_uraw", [P, 2, QUAD * P])
            f_u = pair(s, "f_u", [P, 2, QUAD * P])

        started = ctx.enter_context(nc.semaphore("started"))
        waits_over = {eng.engine: sem(f"waits_over{i}") for i, eng in enumerate((nc.sync, nc.tensor, nc.vector, nc.gpsimd))}
        ident_in = sem("ident_in"); zero_set = sem("zero_set"); pads_out = sem("pads_out")
        c_small_in = sem("c_small_in"); c_wq_in = sem("c_wq_in"); c_wk_in = sem("c_wk_in")
        c_wv_in = sem("c_wv_in"); c_wo_in = sem("c_wo_in"); c_x_in = [sem(f"c_x_in{i}") for i in range(QUAD)]
        c_bk_set = sem("c_bk_set"); c_q_mm = sem("c_q_mm"); c_q_set = sem("c_q_set"); c_A_mm = sem("c_A_mm")
        c_A_set = sem("c_A_set"); c_wvo_hi = sem("c_wvo_hi"); c_wvo_lo = sem("c_wvo_lo"); c_Ab_hi = sem("c_Ab_hi")
        c_Ab_lo = sem("c_Ab_lo"); c_xT_mm = sem("c_xT_mm"); c_xT_hi = sem("c_xT_hi"); c_xT_lo = sem("c_xT_lo")
        c_v_mm = sem("c_v_mm"); c_att_add = sem("c_att_add"); c_att_set = sem("c_att_set"); c_v_biased = sem("c_v_biased")
        c_ctx_set = sem("c_ctx_set"); c_ctxT_mm = sem("c_ctxT_mm"); c_ctxT_hi = sem("c_ctxT_hi")
        c_ctxT_lo = sem("c_ctxT_lo"); c_o_mm = sem("c_o_mm"); c_o_set = sem("c_o_set")
        c_stored = [sem(f"c_stored{i}") for i in range(2)]
        a_const_in = sem("a_const_in"); a_scale_in = sem("a_scale_in"); a_rope_in = sem("a_rope_in")
        a_stage_in = [sem(f"a_stage_in{i}") for i in range(2)]
        a_w_hi = sem("a_w_hi"); a_w_lo = sem("a_w_lo"); a_rope_set = sem("a_rope_set"); a_carry_zero = sem("a_carry_zero")
        a_h_in = [sem(f"a_h_in{i}") for i in range(QUAD)]; a_res_in = [sem(f"a_res_in{i}") for i in range(2)]
        a_hT_mm = sem("a_hT_mm"); a_hT_hi = sem("a_hT_hi"); a_hT_lo = sem("a_hT_lo")
        a_q_mm = sem("a_q_mm"); a_k_mm = sem("a_k_mm"); a_v_mm = sem("a_v_mm")
        a_q_copied = sem("a_q_copied"); a_squared = sem("a_squared"); a_ss_set = sem("a_ss_set")
        a_rs_step = sem("a_rs_step"); a_norms_set = sem("a_norms_set"); a_krot_step = sem("a_krot_step")
        a_rot_step = sem("a_rot_step"); a_q_rotated = sem("a_q_rotated"); a_k_rotated = sem("a_k_rotated")
        a_QT_mm = sem("a_QT_mm"); a_QT_hi = sem("a_QT_hi"); a_QT_lo = sem("a_QT_lo")
        a_KT_mm = sem("a_KT_mm"); a_KT_hi = sem("a_KT_hi"); a_KT_lo = sem("a_KT_lo")
        a_V_hi = sem("a_V_hi"); a_V_lo = sem("a_V_lo"); a_carried = sem("a_carried"); a_mask_set = sem("a_mask_set")
        a_S_mm = sem("a_S_mm"); a_S_masked = sem("a_S_masked");
        a_exp = sem("a_exp"); a_inv_set = sem("a_inv_set"); a_P_set = sem("a_P_set")
        a_PT_mm = sem("a_PT_mm"); a_PT_hi = sem("a_PT_hi"); a_PT_lo = sem("a_PT_lo")
        a_O_mm = sem("a_O_mm"); a_O_hi = sem("a_O_hi"); a_O_lo = sem("a_O_lo")
        a_wo_mm = sem("a_wo_mm"); a_out_set = sem("a_out_set"); a_stored = [sem(f"a_stored{i}") for i in range(2)]
        f_small_in = sem("f_small_in"); f_stage1_in = [sem(f"f_stage1_in{i}") for i in range(2)]
        f_stage2_in = [sem(f"f_stage2_in{i}") for i in range(2)]
        f_w1_step = sem("f_w1_step"); f_w1_hi = sem("f_w1_hi"); f_w1_lo = sem("f_w1_lo"); f_w2_hi = sem("f_w2_hi"); f_w2_lo = sem("f_w2_lo")
        f_h_in = sem("f_h_in"); f_res_in = [sem(f"f_res_in{i}") for i in range(2)]
        f_ln_step = sem("f_ln_step"); f_h_normed = sem("f_h_normed")
        f_hT_mm = sem("f_hT_mm"); f_hT_raw = sem("f_hT_raw"); f_hT_hi = sem("f_hT_hi"); f_hT_lo = sem("f_hT_lo")
        f_a_mm = sem("f_a_mm"); f_g_mm = sem("f_g_mm"); f_gelu = sem("f_gelu"); f_u_raw = sem("f_u_raw")
        f_u_hi = sem("f_u_hi"); f_u_lo = sem("f_u_lo"); f_w2_mm = sem("f_w2_mm"); f_res_step = sem("f_res_step")
        f_out_set = sem("f_out_set"); f_stored = [sem(f"f_stored{i}") for i in range(2)]
        f_last_set = sem("f_last_set"); a_over = sem("a_over")

        PREPS = TILES + 1
        HTS = TILES + 2
        SPLIT_BY_ACT = 3
        FHTS = (BLOCKS + 1) * KT_
        pt_bank = (2, 3, 7)

        def row_of(block, tile):
            return (block * QUAD + tile) * P + block // BPB

        def load_shifted(sp, src, dst, row, done):
            sp.dma_start(dst[:, 0:HALF], src[bass.ds(row + 1, P), 0:HALF]).then_inc(done, 16)
            sp.dma_start(dst[:, HALF:D], src[bass.ds(row, P), HALF:D]).then_inc(done, 16)

        def load_shifted_block(eng, src, dst, row, done):
            for half, first in ((slice(0, HALF), row + 1), (slice(HALF, D), row)):
                eng.dma_start(dst[:, :, half], src[bass.ds(first, QUAD * P), half].rearrange("(j p) d -> p j d", p=P))\
                   .then_inc(done, 16)

        def stage_up(eng, l, m):
            for side in range(2):
                c0 = side * HID + m * P
                eng.dma_start(f_stage1[:, m % 2, side, :, 0:ROWS[m]],
                              w1[bass.ds(l, 1), :, c0:c0 + ROWS[m]].rearrange("a (k p) n -> p (a k) n", p=P))\
                   .then_inc(f_stage1_in[m % 2], 16)

        def stage_down(eng, l, m):
            eng.dma_start(f_stage2[0:ROWS[m], m % 2, :],
                          w2[bass.ds(l, 1), m * P:m * P + ROWS[m], :].rearrange("a p n -> (a p) n"))\
               .then_inc(f_stage2_in[m % 2], 16)

        def waits_end(eng):
            eng.sem_inc(waits_over[eng.engine], 1)

        def three_passes(pe, dst, w, m, start, stop):
            pe.matmul(dst, w[0], m[0], start=start, stop=False)
            pe.matmul(dst, w[0], m[1], start=False, stop=False)
            return pe.matmul(dst, w[1], m[0], start=False, stop=stop)

        ctx.enter_context(nc.allow_non_contiguous_dma(reason="small vectors laid along the partitions"))
        block = ctx.enter_context(nc.Block())

        @block.sync
        def _(sp):
            def condition():
                sp.dma_start(ident[:], ident_dram).then_inc(ident_in, 16)
                for r in range(QUAD):
                    sp.dma_start(c_x[:, r, :], x_rows[r * P:(r + 1) * P, :]).then_inc(c_x_in[r], 16)
                sp.dma_start(c_wq[:], wqT.rearrange("(k p) n -> p k n", p=P)).then_inc(c_wq_in, 16)
                sp.dma_start(c_cond[:], cond).then_inc(c_small_in, 16)
                sp.dma_start(c_bq[:], bq.rearrange("(k p) -> p k", p=P)).then_inc(c_small_in, 16)
                sp.dma_start(c_bk[:], bk.rearrange("(k p) -> p k", p=P)).then_inc(c_small_in, 16)
                sp.dma_start(c_headmask[:], headmask_dram.rearrange("p (k h) -> p k h", k=KT_)).then_inc(c_small_in, 16)
                sp.dma_start(c_wk[:], wk.rearrange("(k p) n -> p k n", p=P)).then_inc(c_wk_in, 16)
                sp.dma_start(c_wv_raw[:], wvT.rearrange("(k p) n -> p k n", p=P)).then_inc(c_wv_in, 16)
                sp.dma_start(c_bv[:], bv.unsqueeze(0).to_broadcast([P, D])).then_inc(c_small_in, 16)
                sp.dma_start(c_bo[:], bo.unsqueeze(0).to_broadcast([P, D])).then_inc(c_small_in, 16)
                sp.dma_start(c_wo_raw[:], woT.rearrange("(k p) n -> p k n", p=P)).then_inc(c_wo_in, 16)
                sp.wait_ge(zero_set, START + 1)
                for scratch in (x_in, x_mid):
                    for b in range(B):
                        sp.dma_start(scratch[b * BROWS:b * BROWS + 1, :], zero[0:1, :]).then_inc(pads_out, 16)
                    for r in range(QUAD):
                        sp.dma_start(scratch[B * BROWS + r * P:B * BROWS + (r + 1) * P, :], zero[:]).then_inc(pads_out, 16)
                    sp.dma_start(scratch[SROWS - 1:SROWS, :], zero[0:1, :]).then_inc(pads_out, 16)
                for b in range(B):
                    with sp.Fori(0, BPB) as blk:
                        tile0 = (b * BPB + blk) * QUAD
                        for j in range(QUAD):
                            sp.wait_ge(c_o_set, START + tile0 + j + 1)
                            sp.dma_start(x_in[bass.ds(b * BROWS + 1 + (blk * QUAD + j) * P, P), :],
                                         out_tiles[:, j % 2, :]).then_inc(c_stored[j % 2], 16)
                            nxt = (b * BPB + blk + 1) if b + 1 < B else (b * BPB) + (blk + 1) % BPB
                            sp.wait_ge(c_xT_mm, START + tile0 + j + 1)
                            sp.dma_start(c_x[:, j, :], x_rows[bass.ds((nxt * QUAD + j) * P, P), :])\
                              .then_inc(c_x_in[j], 16)
                for i in range(2):
                    sp.wait_ge(c_stored[i], START + TILES // 2 * 16)
                for j in range(QUAD):
                    sp.wait_ge(c_x_in[j], START + (BLOCKS + 1) * 16)
                sp.wait_ge(pads_out, START + 16 * 2 * (B + QUAD + 1))

            def attention(l):
                for i in range(2):
                    sp.wait_ge(f_stored[i], START + l * (TILES // 2 * 32))
                    waits_end(sp)
                sp.wait_ge(f_hT_lo, START + l * FHTS)
                sp.wait_ge(f_hT_hi, START + l * FHTS)
                waits_end(sp)
                for j in range(QUAD):
                    load_shifted(sp, x_in, a_h[:, j, :], row_of(0, j), a_h_in[j])
                for c in range(4):
                    src = wqkv[bass.ds(l, 1), :, c * INNER:(c + 1) * INNER] if c < 3 else wo[bass.ds(l, 1), :, :]
                    if c >= 2:
                        sp.wait_ge(a_w_hi, START + 4 * l + c - 1)
                        sp.wait_ge(a_w_lo, START + 4 * l + c - 1)
                    sp.dma_start(a_stage[c % 2][:], src.rearrange("a (k p) n -> p (a k) n", p=P))\
                      .then_inc(a_stage_in[c % 2], 16)
                    if c == 0:
                        sp.dma_start(a_rope[:], rope_dram.rearrange("p (t c d) -> p t c d", t=TB, c=4)).then_inc(a_rope_in, 16)
                        sp.dma_start(a_masks[:], mask_dram.rearrange("p (v n) -> p v n", v=3)).then_inc(a_const_in, 16)
                        for w, v in ((0, q_scale), (2, k_scale)):
                            row = v[bass.ds(l, 1), :]
                            sp.dma_start(a_qk_scale[:, w, :], row.to_broadcast([P, HD])).then_inc(a_scale_in, 16)
                            sp.dma_start(a_qk_scale[:, w + 1, 0:HD // 2],
                                         row[:, HD // 2:HD].to_broadcast([P, HD // 2])).then_inc(a_scale_in, 16)
                            sp.dma_start(a_qk_scale[:, w + 1, HD // 2:HD],
                                         row[:, 0:HD // 2].to_broadcast([P, HD // 2])).then_inc(a_scale_in, 16)
                sp.dma_start(a_res[:, 0, :], x_in[1:1 + P, :]).then_inc(a_res_in[0], 16)
                def around(blk, j):
                    tile = l * TILES + blk * QUAD + j
                    sp.wait_ge(a_hT_mm, START + l * HTS + blk * QUAD + j + 1)
                    load_shifted(sp, x_in, a_h[:, j, :], row_of(blk + 1, j), a_h_in[j])
                    sp.wait_ge(a_out_set, START + tile)
                    nxt = row_of(blk, j + 1) if j < QUAD - 1 else row_of(blk + 1, 0)
                    sp.dma_start(a_res[:, (j + 1) % 2, :], x_in[bass.ds(nxt + 1, P), :])\
                      .then_inc(a_res_in[(j + 1) % 2], 16)
                    if j == QUAD - 1:
                        sp.wait_ge(a_KT_hi, START + l * PREPS + blk * QUAD + j + 1)
                        sp.wait_ge(a_KT_lo, START + l * PREPS + blk * QUAD + j + 1)
                        sp.wait_ge(a_V_hi, START + l * PREPS + blk * QUAD + j + 1)
                        sp.wait_ge(a_V_lo, START + l * PREPS + blk * QUAD + j + 1)
                        waits_end(sp)
                        sp.wait_ge(a_O_mm, START + tile * H)
                        for part in range(2):
                            keys, values = a_KT[part][:].bitcast(F32), a_V[part][:].bitcast(F32)
                            sp.dma_start(keys[:, :, 0:2 * P], keys[:, :, QUAD * P:SLOTS * P]).then_inc(a_carried, 16)
                            sp.dma_start(values[:, 0:2, :], values[:, QUAD:SLOTS, :]).then_inc(a_carried, 16)

                def stores(blk, j):
                    sp.wait_ge(a_out_set, START + l * TILES + blk * QUAD + j + 1)
                    sp.dma_start(x_mid[bass.ds(row_of(blk, j) + 1, P), :], out_tiles[:, j % 2, :])\
                      .then_inc(a_stored[j % 2], 16)

                with sp.Fori(0, BLOCKS - 1) as blk:
                    for j in range(QUAD):
                        around(blk, j)
                        stores(blk, j)
                for j in range(QUAD - 1):
                    around(BLOCKS - 1, j)
                    stores(BLOCKS - 1, j)
                around(BLOCKS - 1, QUAD - 1)
                for done in (a_q_mm, a_k_mm, a_v_mm):
                    sp.wait_ge(done, START + (l + 1) * PREPS)
                for i in range(2):
                    sp.wait_ge(a_stored[i], START + (l * (TILES // 2) + QUAD // 2) * 16)
                load_shifted_block(sp, x_mid, f_h, row_of(0, 0), f_h_in)
                stage_up(sp, l, 0)
                stage_down(sp, l, 0)
                stage_up(sp, l, 1)
                stage_down(sp, l, 1)
                stores(BLOCKS - 1, QUAD - 1)

            def feed(l):
                for i in range(2):
                    sp.wait_ge(a_res_in[i], START + ((l + 1) * (TILES // 2 * 16 + (16 if i == 0 else 0))))
                    waits_end(sp)
                for j in range(QUAD):
                    sp.wait_ge(a_h_in[j], START + (l + 1) * ((BLOCKS + 1) * 32))
                waits_end(sp)
                sp.wait_ge(a_carried, START + (l + 1) * (BLOCKS * 64))
                waits_end(sp)
                for done in (a_KT_hi, a_KT_lo, a_V_hi, a_V_lo, a_QT_hi, a_QT_lo):
                    sp.wait_ge(done, START + (l + 1) * PREPS)
                waits_end(sp)
                for done in (a_hT_hi, a_hT_lo):
                    sp.wait_ge(done, START + (l + 1) * HTS)
                waits_end(sp)
                sp.wait_ge(a_mask_set, START + (l + 1) * (2 * (BLOCKS + 1)))
                waits_end(sp)
                sp.sem_inc(a_over, 1)
                for w, v in ((0, ln_g), (1, ln_b)):
                    sp.dma_start(f_ln[:, w, :], v[bass.ds(l, 1), :].rearrange("a (k p) -> p (a k)", p=P)).then_inc(f_small_in, 16)
                for m in range(HM):
                    if m >= 2:
                        sp.wait_ge(f_w1_hi, START + HM * l + m - 1)
                        sp.wait_ge(f_w1_lo, START + HM * l + m - 1)
                        sp.wait_ge(f_w2_hi, START + HM * l + m - 1)
                        sp.wait_ge(f_w2_lo, START + HM * l + m - 1)
                    if m >= 2:
                        stage_up(sp, l, m)
                        stage_down(sp, l, m)
                    if m == 0:
                        for side in range(2):
                            c0 = side * HID
                            sp.dma_start(f_b1[:, side, 0:HM - 1],
                                         b1[bass.ds(l, 1), c0:c0 + (HM - 1) * P].rearrange("a (m p) -> p (a m)", p=P))\
                              .then_inc(f_small_in, 16)
                            sp.dma_start(f_b1[0:ROWS[-1], side, HM - 1:HM],
                                         b1[bass.ds(l, 1), c0 + (HM - 1) * P:c0 + HID].rearrange("a p -> p a"))\
                              .then_inc(f_small_in, 16)
                        sp.dma_start(f_b2[:], b2[bass.ds(l, 1), :].to_broadcast([P, D])).then_inc(f_small_in, 16)
                with sp.Fori(0, BLOCKS) as blk:
                    n = l * BLOCKS + blk
                    for j in range(QUAD):
                        if j >= 2:
                            sp.wait_ge(f_out_set, START + n * QUAD + j - 1)
                        sp.dma_start(f_res[:, j % 2, :], x_mid[bass.ds(row_of(blk, j) + 1, P), :])\
                          .then_inc(f_res_in[j % 2], 16)
                        sp.dma_start(f_x[:, j % 2, :], x_rows[bass.ds((blk * QUAD + j) * P, P), :])\
                          .then_inc(f_res_in[j % 2], 16)
                        if j >= 2:
                            store(l, blk, n, j - 2)
                    for j in range(2, QUAD):
                        store(l, blk, n, j)

            def store(l, blk, n, j):
                sp.wait_ge(f_out_set, START + n * QUAD + j + 1)
                sp.dma_start(x_in[bass.ds(row_of(blk, j) + 1, P), :], out_tiles[:, j % 2, :]).then_inc(f_stored[j % 2], 16)
                sp.dma_start(out_rows[bass.ds((blk * QUAD + j) * P, P), :], out_tiles[:, j % 2, :])\
                  .then_inc(f_stored[j % 2], 16)

            sp.wait_ge(started, 1)
            condition()
            with sp.Fori(0, L) as l:
                attention(l)
                feed(l)
            for i in range(2):
                sp.wait_ge(f_stored[i], START + L * (TILES // 2 * 32))
            sp.wait_ge(f_h_in, START + L * (BLOCKS + 1) * 32)

        @block.tensor
        def _(pe):
            def transpose_tile(dst, src):
                for k in range(KT_):
                    mm = pe.transpose(dst[:, k * P:(k + 1) * P], src[:, k * P:(k + 1) * P], ident[:])
                return mm

            def condition():
                pe.wait_ge(ident_in, START + 16)
                pe.wait_ge(c_small_in, START + 6 * 16)
                pe.wait_ge(c_wq_in, START + 16)
                for m in range(KT_):
                    for k in range(KT_):
                        mm = pe.matmul(bank[0][:, m * B:(m + 1) * B], c_wq[:, k, m * P:(m + 1) * P], c_cond[:, k, :],
                                       start=(k == 0), stop=(k == KT_ - 1))
                mm.then_inc(c_q_mm, 1)
                pe.wait_ge(c_q_set, START + 2)
                pe.wait_ge(c_wk_in, START + 16)
                pe.wait_ge(c_bk_set, START + 1)
                for k in range(KT_):
                    for m in range(KT_):
                        mm = pe.matmul(bank[1][:, k * B * CH:(k + 1) * B * CH], c_wk[:, m, k * P:(k + 1) * P],
                                       c_qblk[:, m, :, :].rearrange("p b h -> p (b h)"),
                                       start=(m == 0), stop=(m == KT_ - 1))
                for m in range(KT_):
                    mm = pe.matmul(bank[2][:, 0:B * CH], c_bk_wide[:, m, :],
                                   c_qblk[:, m, :, :].rearrange("p b h -> p (b h)"),
                                   start=(m == 0), stop=(m == KT_ - 1))
                mm.then_inc(c_A_mm, 1)
                for b in range(B):
                    with pe.Fori(0, BPB) as blk:
                        t0 = (b * BPB + blk) * QUAD
                        n0 = b * BPB + blk

                        def x_T(j):
                            pe.wait_ge(c_x_in[j], START + (n0 + 1) * 16)
                            pe.wait_ge(c_xT_lo, START + t0 + j)
                            pe.wait_ge(c_xT_hi, START + t0 + j)
                            transpose_tile(bank[0], c_x[:, j, :]).then_inc(c_xT_mm, 1)

                        def v(j):
                            pe.wait_ge(c_xT_hi, START + t0 + j + 1)
                            pe.wait_ge(c_xT_lo, START + t0 + j + 1)
                            if j < 2:
                                pe.wait_ge(c_ctx_set, START + 2 * t0)
                            else:
                                pe.wait_ge(c_ctx_set, START + 2 * (t0 + j - 1))
                            for half in range(2):
                                for k in range(KT_):
                                    mm = three_passes(pe, bank[2 + 2 * (j % 2) + half][:, 0:CW],
                                                      [c_xT[i][:, j % 2, k, :] for i in range(2)],
                                                      [c_wv[i][:, k, half, :] for i in range(2)],
                                                      k == 0, k == KT_ - 1)
                                mm.then_inc(c_v_mm, 1)

                        def ctx_T(j):
                            pe.wait_ge(c_ctx_set, START + 2 * (t0 + j + 1))
                            pe.wait_ge(c_ctxT_lo, START + t0 + j)
                            pe.wait_ge(c_ctxT_hi, START + t0 + j)
                            transpose_tile(bank[1], c_ctx[:, j % 2, :]).then_inc(c_ctxT_mm, 1)

                        def o(j):
                            pe.wait_ge(c_ctxT_hi, START + t0 + j + 1)
                            pe.wait_ge(c_ctxT_lo, START + t0 + j + 1)
                            if j < 2:
                                pe.wait_ge(c_o_set, START + t0)
                            else:
                                pe.wait_ge(c_o_set, START + t0 + j - 1)
                            for k in range(KT_):
                                mm = three_passes(pe, bank[6 + j % 2][:],
                                                  [c_ctxT[i][:, j % 2, k, :] for i in range(2)],
                                                  [c_wo[i][:, k, :] for i in range(2)], k == 0, k == KT_ - 1)
                            mm.then_inc(c_o_mm, 1)

                        x_T(0)
                        pe.wait_ge(c_Ab_hi, START + b + 1)
                        pe.wait_ge(c_Ab_lo, START + b + 1)
                        pe.wait_ge(c_wvo_hi, START + 2)
                        pe.wait_ge(c_wvo_lo, START + 2)
                        x_T(1)
                        v(0)
                        x_T(2)
                        v(1)
                        ctx_T(0)
                        x_T(3)
                        v(2)
                        ctx_T(1)
                        o(0)
                        v(3)
                        ctx_T(2)
                        o(1)
                        ctx_T(3)
                        o(2)
                        o(3)

            def attention(l):
                q_bank, k_bank, v_bank, o_bank = 4, 5, 6, 7

                def h_T(slot, loads, count):
                    pe.wait_ge(a_h_in[slot], START + loads * 32)
                    pe.wait_ge(a_hT_hi, START + count)
                    pe.wait_ge(a_hT_lo, START + count)
                    transpose_tile(bank[v_bank], a_h[:, slot, :]).then_inc(a_hT_mm, 1)

                def project(which, k, par, done):
                    mm = three_passes(pe, bank[(q_bank, k_bank, v_bank)[which]][:],
                                      [a_hT[i][:, par, k, :] for i in range(2)],
                                      [a_w[which][i][:, k, :] for i in range(2)], k == 0, k == KT_ - 1)
                    if k == KT_ - 1:
                        mm.then_inc(done, 1)

                def q_T(count):
                    pe.wait_ge(a_q_rotated, START + count + 1)
                    pe.wait_ge(a_squared, START + 2 * count + 1)
                    transpose_tile(bank[q_bank], a_qrot[:]).then_inc(a_QT_mm, 1)

                def k_T(count):
                    pe.wait_ge(a_k_rotated, START + count + 1)
                    transpose_tile(bank[k_bank], a_krot[:]).then_inc(a_KT_mm, 1)

                pe.wait_ge(a_O_hi, START + l * TILES * H)
                h_T(0, (BLOCKS + 1) * l + 1, l * HTS)
                h_T(1, (BLOCKS + 1) * l + 1, l * HTS + 1)
                for which, done in ((0, a_q_mm), (1, a_k_mm), (2, a_v_mm)):
                    pe.wait_ge(a_w_hi, START + 4 * l + which + 1)
                    pe.wait_ge(a_w_lo, START + 4 * l + which + 1)
                    if which == 2:
                        pe.wait_ge(a_hT_hi, START + l * HTS + 2)
                        pe.wait_ge(a_hT_lo, START + l * HTS + 2)
                    for k in range(KT_):
                        project(which, k, 0, done)
                q_T(l * PREPS)
                k_T(l * PREPS)
                pe.wait_ge(a_w_hi, START + 4 * l + 4)
                pe.wait_ge(a_w_lo, START + 4 * l + 4)
                pe.wait_ge(a_carry_zero, START + 4 * l + 4)
                waits_end(pe)
                with pe.Fori(0, BLOCKS) as blk:
                    for j in range(QUAD):
                        tile = l * TILES + blk * QUAD + j
                        prep = l * PREPS + blk * QUAD + j
                        ht = l * HTS + blk * QUAD + j
                        par = j % 2

                        def scores(h):
                            r = slice((h % 2) * HD, (h % 2) * HD + HD)
                            if h >= 2:
                                pe.wait_ge(a_S_masked, START + tile * H + h - 1)
                            three_passes(pe, bank[h % 2][:, 0:WIN * P],
                                         [a_QT[i][r, par, h // 2, :] for i in range(2)],
                                         [a_KT[i][r, h // 2, j * P:(j + WIN) * P] for i in range(2)],
                                         True, True).then_inc(a_S_mm, 1)

                        def p_T(h):
                            pe.wait_ge(a_P_set, START + tile * H + h + 1)
                            if h == 2:
                                pe.wait_ge(a_out_set, START + tile)
                            if h >= 3:
                                pe.wait_ge(a_O_hi, START + tile * H + h - 2)
                                pe.wait_ge(a_O_lo, START + tile * H + h - 2)
                            for kb in range(WIN):
                                mm = pe.transpose(bank[pt_bank[h % 3]][:, kb * P:(kb + 1) * P],
                                                  a_P[:, h % 3, kb * P:(kb + 1) * P], ident[:])
                            mm.then_inc(a_PT_mm, 1)

                        def pv(h):
                            pe.wait_ge(a_PT_hi, START + tile * H + h + 1)
                            pe.wait_ge(a_PT_lo, START + tile * H + h + 1)
                            for kb in range(WIN):
                                mm = three_passes(pe, bank[pt_bank[h % 3]][0:HD, WIN * P:WIN * P + P],
                                                  [a_V[i][:, j + kb, h * HD:(h + 1) * HD] for i in range(2)],
                                                  [a_PT[i][:, h % 2, kb * P:(kb + 1) * P] for i in range(2)],
                                                  kb == 0, kb == WIN - 1)
                            mm.then_inc(a_O_mm, 1)

                        work = [[(0, 0), (0, 1), (0, 2)], [(0, 3), (1, 0)], [(1, 1), (1, 2)], [(1, 3)],
                                [(2, 0)], [(2, 1)], [(2, 2)], [(2, 3)]]
                        if j == 0:
                            pe.wait_ge(a_carried, START + (l * BLOCKS + blk) * 64)
                        pe.wait_ge(a_S_masked, START + tile * H)
                        pe.wait_ge(a_O_hi, START + tile * H)
                        pe.wait_ge(a_O_lo, START + tile * H)
                        for ready in (a_V_hi, a_V_lo, a_QT_hi, a_QT_lo, a_KT_hi, a_KT_lo):
                            pe.wait_ge(ready, START + prep + 1)
                        scores(0)
                        scores(1)
                        pe.wait_ge(a_hT_hi, START + ht + 2)
                        pe.wait_ge(a_hT_lo, START + ht + 2)
                        for h in range(H):
                            if 0 < h < H - 2:
                                scores(h + 2)
                            for which, k in work[h]:
                                project(which, k, 1 - par, (a_q_mm, a_k_mm, a_v_mm)[which])
                            if h == 0:
                                scores(2)
                            if h == H - 1:
                                q_T(prep + 1)
                            p_T(h)
                            if h >= 1:
                                pv(h - 1)

                        def project_out(k):
                            pe.wait_ge(a_O_hi, START + (tile * H + (2 * k + 2 if k >= 3 else 6)))
                            pe.wait_ge(a_O_lo, START + (tile * H + (2 * k + 2 if k >= 3 else 6)))
                            return three_passes(pe, bank[o_bank][:], [a_OT[i][:, par, k, :] for i in range(2)],
                                                [a_w[3][i][:, k, :] for i in range(2)], k == 0, k == PAIRS - 1)

                        project_out(0)
                        project_out(1)
                        pv(H - 1)
                        pe.wait_ge(a_V_hi, START + prep + 2)
                        pe.wait_ge(a_V_lo, START + prep + 2)
                        slot = (j + 2) % QUAD
                        h_T(slot, (BLOCKS + 1) * l + blk + (j + 2) // QUAD + 1, ht + 2)
                        k_T(prep + 1)
                        project_out(2)
                        mm = project_out(3)
                        mm.then_inc(a_wo_mm, 1)

            def feed(l):
                def h_T(k, dst):
                    for j in range(QUAD):
                        mm = pe.transpose(dst[:, j * P:(j + 1) * P], f_h[:, j, k * P:(k + 1) * P], ident[:])
                    mm.then_inc(f_hT_mm, 1)

                a_bank, g_bank = (4, 6), (5, 7)
                pe.wait_ge(f_h_normed, START + (l * (BLOCKS + 1) + 1) * QUAD)
                for k in range(KT_):
                    h_T(k, bank[4 + k])
                with pe.Fori(0, BLOCKS) as blk:
                    n = l * BLOCKS + blk
                    pe.wait_ge(f_hT_hi, START + l * FHTS + blk * KT_ + KT_)
                    pe.wait_ge(f_hT_lo, START + l * FHTS + blk * KT_ + KT_)

                    def up(m):
                        if m >= 2:
                            pe.wait_ge(f_u_raw, START + n * HM + m - 1)
                        for which, dst, done in ((0, a_bank[m % 2], f_a_mm), (1, g_bank[m % 2], f_g_mm)):
                            pe.wait_ge(f_w1_hi, START + l * HM + m + 1)
                            pe.wait_ge(f_w1_lo, START + l * HM + m + 1)
                            c0 = which * HID + m * P
                            for k in range(KT_):
                                mm = three_passes(pe, bank[dst][0:ROWS[m], :],
                                                  [f_w1[i][:, k, c0:c0 + ROWS[m]] for i in range(2)],
                                                  [f_hT[i][:, k, :] for i in range(2)], k == 0, k == KT_ - 1)
                            mm.then_inc(done, 1)

                    def down(m):
                        pe.wait_ge(f_u_hi, START + n * HM + m + 1)
                        pe.wait_ge(f_u_lo, START + n * HM + m + 1)
                        pe.wait_ge(f_w2_hi, START + l * HM + m + 1)
                        pe.wait_ge(f_w2_lo, START + l * HM + m + 1)
                        for j in range(QUAD):
                            if m == 0:
                                pe.wait_ge(f_out_set, START + n * QUAD)
                            mm = three_passes(pe, bank[j][:],
                                              [f_u[i][0:ROWS[m], m % 2, j * P:(j + 1) * P] for i in range(2)],
                                              [f_w2[i][0:ROWS[m], m, :] for i in range(2)], m == 0, m == HM - 1)
                        mm.then_inc(f_w2_mm, 1)

                    for m in range(HM):
                        up(m)
                        if m >= 1:
                            down(m - 1)
                    pe.wait_ge(f_h_normed, START + (l * (BLOCKS + 1) + blk + 2) * QUAD)
                    first = (HM - 2) % 2
                    h_T(0, bank[a_bank[first]])
                    h_T(1, bank[g_bank[first]])
                    down(HM - 1)
                    h_T(2, bank[a_bank[1 - first]])
                    h_T(3, bank[g_bank[1 - first]])

            pe.wait_ge(started, 1)
            condition()
            with pe.Fori(0, L) as l:
                attention(l)
                feed(l)

        @block.scalar
        def _(act):
            def condition():
                for n, (raw_in, parts) in enumerate(((c_wv_in, None), (c_wo_in, None))):
                    act.wait_ge(raw_in, START + 16)
                    if n == 0:
                        for half in range(2):
                            cp = act.activation(c_wv[0][:, :, half, 0:HALF],
                                                c_wv_raw[:, :, half * HALF:(half + 1) * HALF], ACT.Copy)
                    else:
                        cp = act.activation(c_wo[0][:], c_wo_raw[:], ACT.Copy)
                    cp.then_inc(c_wvo_hi, 1)
                for b in range(B):
                    act.wait_ge(c_A_set, START + 1)
                    if b > 0:
                        act.wait_ge(c_v_mm, START + 2 * b * TB)
                    for half in range(2):
                        cp = act.activation(c_wv[0][:, :, half, HALF:CW],
                                            c_A[:, :, b * CH + half * (CH // 2):b * CH + (half + 1) * (CH // 2)], ACT.Copy)
                    cp.then_inc(c_Ab_hi, 1)
                    with act.Fori(0, BPB) as blk:
                        t0 = (b * BPB + blk) * QUAD

                        def x_T(j):
                            act.wait_ge(c_xT_mm, START + t0 + j + 1)
                            act.wait_ge(c_v_mm, START + (2 * (t0 if j < 2 else t0 + j - 1)))
                            act.activation(c_xT[0][:, j % 2, :, :], bank[0][:].rearrange("p (k n) -> p k n", k=KT_),
                                           ACT.Copy).then_inc(c_xT_hi, 1)

                        def ctx_T(j):
                            act.wait_ge(c_ctxT_mm, START + t0 + j + 1)
                            act.wait_ge(c_o_mm, START + (t0 if j < 2 else t0 + j - 1))
                            act.activation(c_ctxT[0][:, j % 2, :, :], bank[1][:].rearrange("p (k n) -> p k n", k=KT_),
                                           ACT.Copy).then_inc(c_ctxT_hi, 1)

                        x_T(0)
                        x_T(1)
                        x_T(2)
                        ctx_T(0)
                        x_T(3)
                        ctx_T(1)
                        ctx_T(2)
                        ctx_T(3)

            def attention(l):
                def square(which, count):
                    act.wait_ge((a_q_mm, a_k_mm)[which], START + count + 1)
                    act.wait_ge(a_ss_set, START + 2 * count)
                    act.activation(a_sq[:, which, :], bank[4 + which][:], ACT.Square).then_inc(a_squared, 1)

                def q_copy(count):
                    act.wait_ge(a_q_mm, START + count + 1)
                    act.wait_ge(a_q_rotated, START + count)
                    act.activation(a_qraw[:], bank[4][:], ACT.Copy).then_inc(a_q_copied, 1)

                def q_T(count, par):
                    act.wait_ge(a_QT_mm, START + count + 1)
                    act.activation(a_QT[0][:, par, :, :], bank[4][:].rearrange("p (c n) -> p c n", c=PAIRS),
                                   ACT.Copy).then_inc(a_QT_hi, 1)

                def k_T(count, slot, used):
                    act.wait_ge(a_KT_mm, START + count + 1)
                    act.wait_ge(a_O_mm, START + used)
                    act.activation(a_KT[0][:, :, slot * P:(slot + 1) * P], bank[5][:].rearrange("p (c n) -> p c n", c=PAIRS),
                                   ACT.Copy).then_inc(a_KT_hi, 1)

                def value(count, slot, used):
                    act.wait_ge(a_v_mm, START + count + 1)
                    act.wait_ge(a_O_mm, START + used)
                    act.activation(a_V[0][:, slot, :], bank[6][:], ACT.Copy).then_inc(a_V_hi, 1)

                def h_T(count, par):
                    act.wait_ge(a_hT_mm, START + count + 1)
                    act.activation(a_hT[0][:, par, :, :], bank[6][:].rearrange("p (k n) -> p k n", k=KT_),
                                   ACT.Copy).then_inc(a_hT_hi, 1)

                h_T(l * HTS, 0)
                h_T(l * HTS + 1, 1)
                for c in range(4):
                    act.wait_ge(a_stage_in[c % 2], START + (2 * l + c // 2 + 1) * 16)
                    act.activation(a_w[c][0][:], a_stage[c % 2][:], ACT.Copy).then_inc(a_w_hi, 1)
                act.wait_ge(a_w_lo, START + 4 * l + 4)
                q_copy(l * PREPS)
                square(0, l * PREPS)
                square(1, l * PREPS)
                value(l * PREPS, WIN - 1, l * TILES * H)
                q_T(l * PREPS, 0)
                k_T(l * PREPS, WIN - 1, l * TILES * H)
                with act.Fori(0, BLOCKS) as blk:
                    for j in range(QUAD):
                        tile = l * TILES + blk * QUAD + j
                        prep = l * PREPS + blk * QUAD + j
                        ht = l * HTS + blk * QUAD + j
                        par = j % 2
                        slot = j + WIN if j < QUAD - 1 else WIN - 1

                        def exp(h):
                            act.wait_ge(a_S_masked, START + tile * H + h + 1)
                            act.wait_ge(a_PT_mm, START + (tile * H + h - 2 if h >= 3 else tile * H))
                            act.activation(a_P[:, h % 3, :], a_S[:, h % 2, :], ACT.Exp, bias=a_bias[:, h % 2:h % 2 + 1],
                                           scale=-1.0, accum_out=a_sum[:, h % 3:h % 3 + 1]).then_inc(a_exp, 1)

                        def normalize(h):
                            act.wait_ge(a_inv_set, START + tile * H + h + 1)
                            act.activation(a_P[:, h % 3, :], a_P[:, h % 3, :], ACT.Copy, scale=a_inv[:, h % 3:h % 3 + 1])\
                               .then_inc(a_P_set, 1)

                        def p_T(h):
                            act.wait_ge(a_PT_mm, START + tile * H + h + 1)
                            act.wait_ge(a_O_mm, START + (tile * H + h - 1 if h >= 2 else tile * H))
                            act.activation(a_PT[0][:, h % 2, :], bank[pt_bank[h % 3]][:, 0:WIN * P], ACT.Copy).then_inc(a_PT_hi, 1)

                        def o_T(h):
                            r = slice((h % 2) * HD, (h % 2) * HD + HD)
                            act.wait_ge(a_O_mm, START + tile * H + h + 1)
                            if h == 0:
                                act.wait_ge(a_wo_mm, START + tile)
                            act.activation(a_OT[0][r, par, h // 2, :], bank[pt_bank[h % 3]][0:HD, WIN * P:WIN * P + P],
                                           ACT.Copy).then_inc(a_O_hi, 1)

                        exp(0)
                        exp(1)
                        normalize(0)
                        for h in range(H):
                            if h >= 2:
                                o_T(h - 2)
                            if h + 1 < H:
                                normalize(h + 1)
                            if h == 2:
                                q_copy(prep + 1)
                                square(0, prep + 1)
                            if h == 4:
                                square(1, prep + 1)
                            if h == H - 1:
                                q_T(prep + 1, 1 - par)
                            p_T(h)
                            if h + 2 < H:
                                exp(h + 2)
                        value(prep + 1, slot, tile * H)
                        o_T(H - 2)
                        o_T(H - 1)
                        h_T(ht + 2, par)
                        k_T(prep + 1, slot, tile * H)

            def feed(l):
                act.wait_ge(a_over, START + l + 1)
                for m in range(SPLIT_BY_ACT):
                    act.wait_ge(f_stage1_in[m % 2], START + (l * ((HM + 1 - m % 2) // 2) + m // 2 + 1) * 32)
                    for side in range(2):
                        act.activation(f_w1[0][:, :, side * HID + m * P:side * HID + m * P + ROWS[m]],
                                       f_stage1[:, m % 2, side, :, 0:ROWS[m]], ACT.Copy).then_inc(f_w1_step, 1)
                    act.wait_ge(f_stage2_in[m % 2], START + (l * ((HM + 1 - m % 2) // 2) + m // 2 + 1) * 16)
                    act.activation(f_w2[0][0:ROWS[m], m, :], f_stage2[0:ROWS[m], m % 2, :], ACT.Copy).then_inc(f_w2_hi, 1)
                act.wait_ge(f_small_in, START + (l + 1) * (7 * 16))
                for i in range(2):
                    act.wait_ge(a_stored[i], START + (l + 1) * (TILES // 2 * 16))
                for k in range(KT_):
                    act.wait_ge(f_hT_raw, START + l * FHTS + k + 1)
                    act.activation(f_hT[0][:, k, :], f_hraw[:, k % 2, :], ACT.Copy).then_inc(f_hT_hi, 1)
                with act.Fori(0, BLOCKS) as blk:
                    n = l * BLOCKS + blk
                    act.wait_ge(f_hT_mm, START + l * FHTS + blk * KT_ + KT_)
                    load_shifted_block(act, x_mid, f_h, row_of(blk + 1, 0), f_h_in)

                    def h_T(k):
                        act.wait_ge(f_hT_raw, START + l * FHTS + (blk + 1) * KT_ + k + 1)
                        if k == 0:
                            act.wait_ge(f_g_mm, START + (n + 1) * HM)
                        act.activation(f_hT[0][:, k, :], f_hraw[:, k % 2, :], ACT.Copy).then_inc(f_hT_hi, 1)

                    for m in range(HM):
                        act.wait_ge(f_g_mm, START + n * HM + m + 1)
                        act.wait_ge(f_u_raw, START + (n * HM + m - 1 if m >= 2 else n * HM))
                        act.activation(f_gate[0:ROWS[m], m % 2, :], bank[5 + 2 * (m % 2)][0:ROWS[m], :], ACT.Gelu,
                                       bias=f_b1[0:ROWS[m], 1, m:m + 1]).then_inc(f_gelu, 1)
                        act.wait_ge(f_u_raw, START + n * HM + m + 1)
                        act.wait_ge(f_w2_mm, START + (n * HM + m - 1 if m >= 2 else n * HM))
                        act.activation(f_u[0][0:ROWS[m], m % 2, :], f_uraw[0:ROWS[m], m % 2, :], ACT.Copy)\
                           .then_inc(f_u_hi, 1)
                    for k in range(KT_):
                        h_T(k)

            act.wait_ge(started, 1)
            condition()
            with act.Fori(0, L) as l:
                attention(l)
                feed(l)

        @block.vector
        def _(dve):
            def condition():
                dve.memset(zero[:], 0.0).then_inc(zero_set, 1)
                dve.memset(f_last_cell[:], -1.0).then_inc(f_last_set, 1)
                dve.wait_ge(c_small_in, START + 6 * 16)
                dve.tensor_copy(c_bk_wide[:], c_bk[:].unsqueeze(2).to_broadcast([P, KT_, P])).then_inc(c_bk_set, 1)
                dve.wait_ge(c_q_mm, START + 1)
                dve.tensor_tensor(c_qT[:], bank[0][:, 0:KT_ * B].rearrange("p (k b) -> p k b", k=KT_),
                                  c_bq[:].unsqueeze(2).to_broadcast([P, KT_, B]), ALU.add).then_inc(c_q_set, 1)
                dve.wait_ge(c_q_set, START + 1)
                dve.tensor_tensor(c_qblk[:], c_headmask[:].unsqueeze(2).to_broadcast([P, KT_, B, CH]),
                                  c_qT[:].unsqueeze(3).to_broadcast([P, KT_, B, CH]), ALU.mult).then_inc(c_q_set, 1)
                dve.wait_ge(c_A_mm, START + 1)
                dve.tensor_copy(c_A[:], bank[1][:, 0:KT_ * B * CH].rearrange("p (k n) -> p k n", k=KT_))
                dve.tensor_copy(c_c[:], bank[2][:, 0:B * CH]).then_inc(c_A_set, 1)
                for n in range(2):
                    dve.wait_ge(c_wvo_hi, START + n + 1)
                    if n == 0:
                        for half in range(2):
                            lo = dve.tensor_tensor(c_wv[1][:, :, half, 0:HALF], c_wv_raw[:, :, half * HALF:(half + 1) * HALF],
                                                   c_wv[0][:, :, half, 0:HALF], ALU.subtract)
                    else:
                        lo = dve.tensor_tensor(c_wo[1][:], c_wo_raw[:], c_wo[0][:], ALU.subtract)
                    lo.then_inc(c_wvo_lo, 1)
                dve.wait_ge(c_A_set, START + 1)
                for b in range(B):
                    dve.wait_ge(c_Ab_hi, START + b + 1)
                    for half in range(2):
                        lo = dve.tensor_tensor(c_wv[1][:, :, half, HALF:CW],
                                               c_A[:, :, b * CH + half * (CH // 2):b * CH + (half + 1) * (CH // 2)],
                                               c_wv[0][:, :, half, HALF:CW], ALU.subtract)
                    lo.then_inc(c_Ab_lo, 1)
                    with dve.Fori(0, BPB) as blk:
                        t0 = (b * BPB + blk) * QUAD

                        def x_T(j):
                            dve.wait_ge(c_xT_hi, START + t0 + j + 1)
                            dve.tensor_tensor(c_xT[1][:, j % 2, :, :], bank[0][:].rearrange("p (k n) -> p k n", k=KT_),
                                              c_xT[0][:, j % 2, :, :], ALU.subtract).then_inc(c_xT_lo, 1)

                        def context(j):
                            dve.wait_ge(c_v_mm, START + 2 * (t0 + j + 1))
                            par = j % 2
                            vb = [bank[2 + 2 * par], bank[3 + 2 * par]]
                            for half in range(2):
                                hs = slice(half * (CH // 2), (half + 1) * (CH // 2))
                                dve.tensor_tensor(c_att[:, par, hs], vb[half][:, HALF:CW],
                                                  c_c[:, b * CH + half * (CH // 2):b * CH + (half + 1) * (CH // 2)],
                                                  ALU.add).then_inc(c_att_add, 1)
                            for half in range(2):
                                cs = slice(half * HALF, (half + 1) * HALF)
                                dve.tensor_tensor(c_tmp[:, par, cs], vb[half][:, 0:HALF], c_bv[:, cs], ALU.add)\
                                   .then_inc(c_v_biased, 1)
                            dve.wait_ge(c_att_add, START + 2 * (t0 + j + 1))
                            dve.tensor_scalar(c_att[:, par, :], c_att[:, par, :], 0.0, 1.0, ALU.max, ALU.min)\
                               .then_inc(c_att_set, 1)
                            dve.wait_ge(c_v_biased, START + 2 * (t0 + j + 1))
                            dve.wait_ge(c_att_set, START + t0 + j + 1)
                            dve.wait_ge(c_ctxT_mm, START + (t0 if j < 2 else t0 + j - 1))
                            dve.tensor_tensor(c_ctx[:, par, :].rearrange("p (h d) -> p h d", h=CH),
                                              c_tmp[:, par, :].rearrange("p (h d) -> p h d", h=CH),
                                              c_att[:, par, :].unsqueeze(2).to_broadcast([P, CH, CHD]), ALU.mult)\
                               .then_inc(c_ctx_set, 2)

                        def ctx_T(j):
                            dve.wait_ge(c_ctxT_hi, START + t0 + j + 1)
                            dve.tensor_tensor(c_ctxT[1][:, j % 2, :, :], bank[1][:].rearrange("p (k n) -> p k n", k=KT_),
                                              c_ctxT[0][:, j % 2, :, :], ALU.subtract).then_inc(c_ctxT_lo, 1)

                        def o(j):
                            dve.wait_ge(c_o_mm, START + t0 + j + 1)
                            dve.wait_ge(c_stored[j % 2], START + (t0 // 2 + j // 2) * 16)
                            dve.tensor_tensor(out_tiles[:, j % 2, :], bank[6 + j % 2][:], c_bo[:], ALU.add).then_inc(c_o_set, 1)

                        x_T(0)
                        x_T(1)
                        context(0)
                        x_T(2)
                        context(1)
                        ctx_T(0)
                        x_T(3)
                        context(2)
                        ctx_T(1)
                        o(0)
                        context(3)
                        ctx_T(2)
                        o(1)
                        ctx_T(3)
                        o(2)
                        o(3)

            def attention(l):
                def sums(count, which):
                    dve.wait_ge(a_squared, START + 2 * count + which + 1)
                    dve.wait_ge(a_norms_set, START + count)
                    dve.tensor_reduce(a_ss[:, which * H:(which + 1) * H], a_sq[:, which, :].rearrange("p (h d) -> p h d", d=HD),
                                      AX_X, ALU.add).then_inc(a_ss_set, 1)

                def rotate_k(count, at, steps=(0, 1, 2)):
                    halves = lambda a: a.rearrange("p (h t d) -> p h t d", h=H, t=2)
                    table = lambda c: a_rope[:, bass.ds(at, 1), 2 + c, :].rearrange("p a (t d) -> p a t d", t=2)\
                        .to_broadcast([P, H, 2, HD // 2])
                    if 0 in steps:
                        dve.wait_ge(a_squared, START + 2 * (count + 1))
                        dve.tensor_tensor(halves(a_kn[:]), halves(bank[5][:])[:, :, ::-1, :], table(1), ALU.mult)\
                           .then_inc(a_krot_step, 1)
                    if 1 in steps:
                        dve.wait_ge(a_KT_mm, START + count)
                        dve.tensor_tensor(halves(a_krot[:]), halves(bank[5][:]), table(0), ALU.mult).then_inc(a_krot_step, 1)
                    if 2 in steps:
                        dve.wait_ge(a_krot_step, START + 3 * count + 2)
                        dve.tensor_tensor(a_krot[:], a_krot[:], a_kn[:], ALU.add).then_inc(a_krot_step, 1)

                def k_norm(count):
                    dve.wait_ge(a_norms_set, START + count + 1)
                    dve.wait_ge(a_krot_step, START + 3 * count + 3)
                    dve.tensor_tensor(a_krot[:].rearrange("p (h d) -> p h d", h=H), a_krot[:].rearrange("p (h d) -> p h d", h=H),
                                      a_rs[:, H:2 * H].unsqueeze(2).to_broadcast([P, H, HD]), ALU.mult).then_inc(a_k_rotated, 1)

                def q_T(count, par):
                    dve.wait_ge(a_QT_hi, START + count + 1)
                    dve.tensor_tensor(a_QT[1][:, par, :, :], bank[4][:].rearrange("p (c n) -> p c n", c=PAIRS),
                                      a_QT[0][:, par, :, :], ALU.subtract).then_inc(a_QT_lo, 1)

                def k_T(count, slot):
                    dve.wait_ge(a_KT_hi, START + count + 1)
                    dve.tensor_tensor(a_KT[1][:, :, slot * P:(slot + 1) * P], bank[5][:].rearrange("p (c n) -> p c n", c=PAIRS),
                                      a_KT[0][:, :, slot * P:(slot + 1) * P], ALU.subtract).then_inc(a_KT_lo, 1)

                def value(count, slot):
                    dve.wait_ge(a_V_hi, START + count + 1)
                    dve.tensor_tensor(a_V[1][:, slot, :], bank[6][:], a_V[0][:, slot, :], ALU.subtract).then_inc(a_V_lo, 1)

                def h_T(count, par):
                    dve.wait_ge(a_hT_hi, START + count + 1)
                    dve.tensor_tensor(a_hT[1][:, par, :, :], bank[6][:].rearrange("p (k n) -> p k n", k=KT_),
                                      a_hT[0][:, par, :, :], ALU.subtract).then_inc(a_hT_lo, 1)

                h_T(l * HTS, 0)
                h_T(l * HTS + 1, 1)
                for c in range(4):
                    dve.wait_ge(a_w_hi, START + 4 * l + c + 1)
                    dve.tensor_tensor(a_w[c][1][:], a_stage[c % 2][:], a_w[c][0][:], ALU.subtract).then_inc(a_w_lo, 1)
                sums(l * PREPS, 0)
                sums(l * PREPS, 1)
                dve.wait_ge(a_rope_set, START + l + 1)
                rotate_k(l * PREPS, 0)
                value(l * PREPS, WIN - 1)
                k_norm(l * PREPS)
                q_T(l * PREPS, 0)
                k_T(l * PREPS, WIN - 1)
                with dve.Fori(0, BLOCKS) as blk:
                    for j in range(QUAD):
                        tile = l * TILES + blk * QUAD + j
                        prep = l * PREPS + blk * QUAD + j
                        ht = l * HTS + blk * QUAD + j
                        par = j % 2
                        slot = j + WIN if j < QUAD - 1 else WIN - 1
                        at = (blk % BPB) * QUAD + j + 1 if j < QUAD - 1 else ((blk + 1) % BPB) * QUAD

                        def mask_max(h):
                            b = h % 2
                            dve.wait_ge(a_exp, START + (tile * H + h - 1 if h >= 2 else tile * H))
                            dve.wait_ge(a_S_mm, START + tile * H + h + 1)
                            if j < 2 and h == 0:
                                dve.wait_ge(a_mask_set, START + (l * (BLOCKS + 1) + blk + 1) * 2)
                            waits_end(dve)
                            dve.tensor_tensor_reduce(a_S[:, b, :], bank[b][:, 0:WIN * P],
                                                     a_mask[:, j, :] if j < 2 else a_masks[:, 2, :],
                                                     a_q8[:, par, h:h + 1], 3.0e38,
                                                     ALU.add, ALU.min, a_bias[:, b:b + 1]).then_inc(a_S_masked, 1)

                        def inverse(h):
                            dve.wait_ge(a_exp, START + tile * H + h + 1)
                            dve.wait_ge(a_P_set, START + (tile * H + h - 2 if h >= 3 else tile * H))
                            dve.reciprocal(a_inv[:, h % 3:h % 3 + 1], a_sum[:, h % 3:h % 3 + 1]).then_inc(a_inv_set, 1)

                        def p_T(h):
                            dve.wait_ge(a_PT_hi, START + tile * H + h + 1)
                            dve.tensor_tensor(a_PT[1][:, h % 2, :], bank[pt_bank[h % 3]][:, 0:WIN * P], a_PT[0][:, h % 2, :],
                                              ALU.subtract).then_inc(a_PT_lo, 1)

                        def o_T(h):
                            r = slice((h % 2) * HD, (h % 2) * HD + HD)
                            dve.wait_ge(a_O_hi, START + tile * H + h + 1)
                            dve.tensor_tensor(a_OT[1][r, par, h // 2, :], bank[pt_bank[h % 3]][0:HD, WIN * P:WIN * P + P],
                                              a_OT[0][r, par, h // 2, :], ALU.subtract).then_inc(a_O_lo, 1)

                        dve.wait_ge(a_norms_set, START + prep + 1)
                        mask_max(0)
                        mask_max(1)
                        inverse(0)
                        inverse(1)
                        for h in range(H):
                            if h >= 2:
                                o_T(h - 2)
                            if h + 2 < H:
                                mask_max(h + 2)
                            if h == 3:
                                sums(prep + 1, 0)
                            if h == 4:
                                sums(prep + 1, 1)
                            if h == 5:
                                rotate_k(prep + 1, at, (0,))
                            if h == 6:
                                rotate_k(prep + 1, at, (1,))
                            if h == 7:
                                rotate_k(prep + 1, at, (2,))
                            if h == 8:
                                k_norm(prep + 1)
                            if h == H - 1:
                                q_T(prep + 1, 1 - par)
                            p_T(h)
                            if h + 2 < H:
                                inverse(h + 2)
                        value(prep + 1, slot)
                        k_norm(prep + 1)
                        o_T(H - 2)
                        o_T(H - 1)
                        h_T(ht + 2, par)
                        k_T(prep + 1, slot)
                        dve.wait_ge(a_wo_mm, START + tile + 1)
                        dve.wait_ge(a_res_in[j % 2],
                                    START + ((l * (TILES // 2 + (1 if j % 2 == 0 else 0)) + blk * (QUAD // 2) + j // 2 + 1) * 16))
                        dve.wait_ge(a_stored[j % 2], START + (l * (TILES // 2) + blk * (QUAD // 2) + j // 2) * 16)
                        dve.tensor_tensor(out_tiles[:, j % 2, :], bank[7][:], a_res[:, j % 2, :], ALU.add).then_inc(a_out_set, 1)

            def feed(l):
                LN = 15 + 2 * QUAD

                def step(k, base, ins):
                    ins.then_inc(f_ln_step, 1)
                    dve.wait_ge(f_ln_step, START + base + k + 1)

                def normalize(count):
                    dve.wait_ge(f_h_in, START + (count + 1) * 32)
                    base = count * LN
                    for j in range(QUAD):
                        dve.bn_stats(f_stats[:, j, :], f_h[:, j, :]).then_inc(f_ln_step, 1)
                    dve.wait_ge(f_ln_step, START + base + QUAD)
                    waits_end(dve)
                    for j in range(QUAD):
                        dve.bn_aggr(f_mv[:, j, :], f_stats[:, j, :]).then_inc(f_ln_step, 1)
                    dve.wait_ge(f_ln_step, START + base + 2 * QUAD)
                    k = 2 * QUAD
                    var, y, t = f_rs[:, 0, :], f_rs[:, 1, :], f_rs[:, 2, :]
                    step(k, base, dve.tensor_scalar(var, f_mv[:, :, 1], 1e-5, None, ALU.add))
                    step(k + 1, base, dve.tensor_scalar(y.bitcast(I32), var.bitcast(I32), -0.5, RSQRT_SEED, ALU.mult, ALU.add))
                    for i in range(4):
                        step(k + 2 + 3 * i, base, dve.tensor_tensor(t, y, y, ALU.mult))
                        step(k + 3 + 3 * i, base, dve.scalar_tensor_tensor(t, t, -0.5, var, ALU.mult, ALU.mult))
                        step(k + 4 + 3 * i, base, dve.scalar_tensor_tensor(y, t, 1.5, y, ALU.add, ALU.mult))
                    step(k + 14, base, dve.memset(t, 0.0))
                    for j in range(QUAD):
                        dve.tensor_scalar(f_h[:, j, :], f_h[:, j, :], f_mv[:, j, 0:1], f_rs[:, 1, j:j + 1],
                                          ALU.subtract, ALU.mult).then_inc(f_h_normed, 1)

                def h_T_raw(count, src, k):
                    dve.wait_ge(f_hT_mm, START + count + 1)
                    if k >= 2:
                        dve.wait_ge(f_hT_lo, START + count - 1)
                    dve.tensor_scalar(f_hraw[:, k % 2, :], src[:], f_ln[:, 0, k:k + 1], f_ln[:, 1, k:k + 1],
                                      ALU.mult, ALU.add).then_inc(f_hT_raw, 1)

                def h_T_lo(count, k):
                    dve.wait_ge(f_hT_hi, START + count + 1)
                    dve.tensor_tensor(f_hT[1][:, k, :], f_hraw[:, k % 2, :], f_hT[0][:, k, :], ALU.subtract)\
                       .then_inc(f_hT_lo, 1)

                dve.wait_ge(f_last_set, START + l + 1)
                dve.tensor_scalar(f_last_cell[:], f_last_cell[:], 1.0, None, ALU.add).then_inc(f_last_set, 1)
                dve.wait_ge(f_last_set, START + l + 2)
                dve.wait_ge(a_over, START + l + 1)
                normalize(l * (BLOCKS + 1))
                dve.wait_ge(f_small_in, START + (l + 1) * (7 * 16))
                for i in range(2):
                    dve.wait_ge(a_stored[i], START + (l + 1) * (TILES // 2 * 16))
                for k in range(KT_):
                    h_T_raw(l * FHTS + k, bank[4 + k], k)
                    h_T_lo(l * FHTS + k, k)
                with dve.Fori(0, BLOCKS) as blk:
                    n = l * BLOCKS + blk
                    nh = l * FHTS + (blk + 1) * KT_

                    def hidden(m):
                        dve.wait_ge(f_gelu, START + n * HM + m + 1)
                        dve.wait_ge(f_a_mm, START + n * HM + m + 1)
                        dve.wait_ge(f_u_hi, START + (n * HM + m - 1 if m >= 2 else n * HM))
                        dve.scalar_tensor_tensor(f_uraw[0:ROWS[m], m % 2, :], bank[4 + 2 * (m % 2)][0:ROWS[m], :],
                                                 f_b1[0:ROWS[m], 0, m:m + 1], f_gate[0:ROWS[m], m % 2, :],
                                                 ALU.add, ALU.mult).then_inc(f_u_raw, 1)
                        dve.wait_ge(f_u_hi, START + n * HM + m + 1)
                        dve.tensor_tensor(f_u[1][0:ROWS[m], m % 2, :], f_uraw[0:ROWS[m], m % 2, :],
                                          f_u[0][0:ROWS[m], m % 2, :], ALU.subtract).then_inc(f_u_lo, 1)

                    def residual(j):
                        s = 2 * (n * QUAD + j)
                        dve.wait_ge(f_res_in[j % 2], START + (n * QUAD // 2 + j // 2 + 1) * 32)
                        dve.scalar_tensor_tensor(f_res[:, j % 2, :], f_x[:, j % 2, :], f_last_cell[:], f_res[:, j % 2, :],
                                                 ALU.mult, ALU.add).then_inc(f_res_step, 1)
                        dve.wait_ge(f_res_step, START + s + 1)
                        dve.tensor_tensor(f_res[:, j % 2, :], f_res[:, j % 2, :], f_b2[:], ALU.add).then_inc(f_res_step, 1)

                    def result(j):
                        dve.wait_ge(f_w2_mm, START + (n + 1) * HM)
                        dve.wait_ge(f_res_step, START + 2 * (n * QUAD + j + 1))
                        dve.wait_ge(f_stored[j % 2], START + (n * QUAD // 2 + j // 2) * 32)
                        dve.tensor_tensor(out_tiles[:, j % 2, :], bank[j][:], f_res[:, j % 2, :], ALU.add).then_inc(f_out_set, 1)

                    for m in range(HM):
                        hidden(m)
                        if m == 3:
                            normalize(l * (BLOCKS + 1) + blk + 1)
                        if m == 5:
                            residual(0)
                            residual(1)
                    first = (HM - 2) % 2
                    h_T_raw(nh, bank[4 + 2 * first], 0)
                    h_T_raw(nh + 1, bank[5 + 2 * first], 1)
                    h_T_lo(nh, 0)
                    h_T_raw(nh + 2, bank[6 - 2 * first], 2)
                    h_T_lo(nh + 1, 1)
                    h_T_raw(nh + 3, bank[7 - 2 * first], 3)
                    h_T_lo(nh + 2, 2)
                    h_T_lo(nh + 3, 3)
                    result(0)
                    result(1)
                    residual(2)
                    result(2)
                    residual(3)
                    result(3)

            dve.wait_ge(started, 1)
            condition()
            with dve.Fori(0, L) as l:
                attention(l)
                feed(l)

        @block.gpsimd
        def _(pool):
            def attention(l):
                RS = 14

                def step(k, base, ins):
                    ins.then_inc(a_rs_step, 1)
                    pool.wait_ge(a_rs_step, START + base + k + 1)

                def norms(count, par):
                    base = count * RS
                    pool.wait_ge(a_ss_set, START + 2 * (count + 1))
                    pool.wait_ge(a_k_rotated, START + count)
                    waits_end(pool)
                    step(0, base, pool.tensor_scalar(a_ss[:], a_ss[:], 1e-24, None, ALU.max))
                    waits_end(pool)
                    step(1, base, pool.tensor_scalar(a_rs[:].bitcast(I32), a_ss[:].bitcast(I32), -0.5, RSQRT_SEED,
                                                     ALU.mult, ALU.add))
                    for i in range(3):
                        step(2 + 4 * i, base, pool.tensor_tensor(a_rt[:], a_rs[:], a_rs[:], ALU.mult))
                        step(3 + 4 * i, base, pool.tensor_tensor(a_rt[:], a_rt[:], a_ss[:], ALU.mult))
                        waits_end(pool)
                        step(4 + 4 * i, base, pool.tensor_scalar(a_rt[:], a_rt[:], -0.5, 1.5, ALU.mult, ALU.add))
                        step(5 + 4 * i, base, pool.tensor_tensor(a_rs[:], a_rs[:], a_rt[:], ALU.mult))
                    waits_end(pool)
                    pool.tensor_scalar(a_q8[:, par, :], a_rs[:, 0:H], -8.0, None, ALU.mult).then_inc(a_norms_set, 1)

                def rotate_q(count, at):
                    halves = lambda a: a.rearrange("p (h t d) -> p h t d", h=H, t=2)
                    table = lambda c: a_rope[:, bass.ds(at, 1), c, :].rearrange("p a (t d) -> p a t d", t=2)\
                        .to_broadcast([P, H, 2, HD // 2])
                    pool.wait_ge(a_q_copied, START + count + 1)
                    pool.wait_ge(a_QT_mm, START + count)
                    pool.tensor_tensor(halves(a_tmp[:]), halves(a_qraw[:])[:, :, ::-1, :], table(1), ALU.mult)\
                        .then_inc(a_rot_step, 1)
                    pool.tensor_tensor(halves(a_qrot[:]), halves(a_qraw[:]), table(0), ALU.mult).then_inc(a_rot_step, 1)
                    pool.wait_ge(a_rot_step, START + 2 * count + 2)
                    pool.tensor_tensor(a_qrot[:], a_qrot[:], a_tmp[:], ALU.add).then_inc(a_q_rotated, 1)

                def masks(first):
                    for t in range(2):
                        at = 2 * first if t == 0 else first + 1
                        pool.tensor_copy(a_mask[:, t, :].rearrange("p (a n) -> p a n", a=1),
                                         a_masks[:, bass.ds(at, 1), :]).then_inc(a_mask_set, 1)

                pool.wait_ge(a_scale_in, START + (l + 1) * (6 * 16))
                pool.wait_ge(a_rope_in, START + (l + 1) * 16)
                pool.tensor_tensor(a_rope[:], a_rope[:], a_qk_scale[:].unsqueeze(1).to_broadcast([P, TB, 4, HD]), ALU.mult)\
                    .then_inc(a_rope_set, 1)
                for part in range(2):
                    pool.memset(a_KT[part][:].bitcast(F32)[:, :, 0:2 * P], 0.0).then_inc(a_carry_zero, 1)
                    pool.memset(a_V[part][:].bitcast(F32)[:, 0:2, :], 0.0).then_inc(a_carry_zero, 1)
                pool.wait_ge(a_const_in, START + (l + 1) * 16)
                waits_end(pool)
                masks(0)
                pool.wait_ge(a_rope_set, START + l + 1)
                rotate_q(l * PREPS, 0)
                norms(l * PREPS, 0)
                with pool.Fori(0, BLOCKS) as blk:
                    for j in range(QUAD):
                        tile = l * TILES + blk * QUAD + j
                        prep = l * PREPS + blk * QUAD + j
                        par = j % 2
                        at = (blk % BPB) * QUAD + j + 1 if j < QUAD - 1 else ((blk + 1) % BPB) * QUAD
                        if j == 2:
                            pool.wait_ge(a_S_masked, START + tile * H)
                            masks(((blk + 1) % BPB + BPB - 1) // BPB)
                        rotate_q(prep + 1, at)
                        pool.wait_ge(a_S_masked, START + tile * H)
                        norms(prep + 1, 1 - par)

            def feed(l):
                for m in range(HM):
                    pool.wait_ge(f_stage1_in[m % 2], START + (l * ((HM + 1 - m % 2) // 2) + m // 2 + 1) * 32)
                    waits_end(pool)
                    wide = lambda part: f_w1[part][:, :, :].rearrange("p k (s n) -> p s k n", s=2)[:, :, :, m * P:m * P + ROWS[m]]
                    raw = f_stage1[:, m % 2, :, :, 0:ROWS[m]]
                    if m >= SPLIT_BY_ACT:
                        for side in range(2):
                            pool.tensor_copy(wide(0)[:, side], raw[:, side]).then_inc(f_w1_step, 1)
                    pool.wait_ge(f_w1_step, START + (l * HM + m + 1) * 2)
                    for side in range(2):
                        lo = pool.tensor_tensor(wide(1)[:, side], raw[:, side], wide(0)[:, side], ALU.subtract)
                        if side == 0:
                            lo.then_inc(f_w1_hi, 1)
                        else:
                            lo.then_inc(f_w1_lo, 1)
                    pool.wait_ge(f_stage2_in[m % 2], START + (l * ((HM + 1 - m % 2) // 2) + m // 2 + 1) * 16)
                    if m >= SPLIT_BY_ACT:
                        waits_end(pool)
                        pool.tensor_copy(f_w2[0][0:ROWS[m], m, :], f_stage2[0:ROWS[m], m % 2, :]).then_inc(f_w2_hi, 1)
                    pool.wait_ge(f_w2_hi, START + l * HM + m + 1)
                    pool.tensor_tensor(f_w2[1][0:ROWS[m], m, :], f_stage2[0:ROWS[m], m % 2, :], f_w2[0][0:ROWS[m], m, :],
                                       ALU.subtract).then_inc(f_w2_lo, 1)

            for s in sems:
                pool.sem_inc(s, START)
            pool.sem_inc(started, 1)
            with pool.Fori(0, L) as l:
                attention(l)
                feed(l)


_INS = ["x", "cond_1024", "L0_cond_Wq", "L0_cond_bq", "L0_cond_Wk", "L0_cond_bk", "L0_cond_Wv", "L0_cond_bv",
        "L0_cond_Wo", "L0_cond_bo", "L0_ffn_wqkv", "L0_ffn_q_scale", "L0_ffn_k_scale", "L0_ffn_wo", "L0_ffn_ln_g",
        "L0_ffn_ln_b", "L0_ffn_w1", "L0_ffn_b1", "L0_ffn_w2", "L0_ffn_b2"]
_TRANSPOSED = ("L0_cond_Wq", "L0_cond_Wv", "L0_cond_Wo")


def kernel(**inputs):
    import concourse.bacc as bacc
    from concourse.bass_utils import run_bass_kernel_spmd

    nc = bacc.Bacc("TRN2", target_bir_lowering=False, num_devices=1)
    arrays, args = {}, []
    for name in _INS:
        a = np.asarray(inputs[name])
        if name == "cond_1024":
            a = a.reshape(a.shape[0], -1, P).transpose(2, 1, 0)
        a = np.ascontiguousarray(a.T if name in _TRANSPOSED else a)
        arrays[f"in_{name}"] = a
        args.append(nc.dram_tensor(f"in_{name}", a.shape, mybir.dt.from_np(a.dtype), kind="ExternalInput").ap())
    shape = tuple(np.asarray(inputs["x"]).shape)
    args.append(nc.dram_tensor("out", shape, F32, kind="ExternalOutput").ap())
    adaln_ffn_program(nc, *args)
    r = run_bass_kernel_spmd(nc, [arrays], core_ids=[0])
    return r.results[0]["out"]
```
